# Optimizing a Trainium2 kernel written in Bass

```python
import numpy as np
import jax
import jax.numpy as jnp

def _softmax(x, axis=-1):
    return jax.nn.softmax(x, axis=axis)

def _gelu(x):
    return jax.nn.gelu(x, approximate=True)

def _silu(x):
    return jax.nn.silu(x)

def _sigmoid(x):
    return jax.nn.sigmoid(x)

def _layernorm(x, axis=-1, eps=1e-05):
    m = jnp.mean(x, axis=axis, keepdims=True)
    v = jnp.var(x, axis=axis, keepdims=True)
    return (x - m) / jnp.sqrt(v + eps)

def _scatter_add(tgt, idx, src, axis=0):
    return tgt.at[idx].add(src)

def _segment_sum(src, seg, n):
    return jax.ops.segment_sum(src, seg, n)
kernel_name = 'mk_gnn_resnorm_d2_gnn_r32_525ce9'

def setup_inputs(seed: int=0):
    np.random.seed(seed)
    _w = jnp.asarray

    def _rec_inputs():
        import jax
        import jax.numpy as jnp
        _gk = jax.random.key(seed)
        x = -0.000202 + 1 * jax.random.normal(jax.random.fold_in(_gk, 1), (50000, 64), jnp.float32)
        src = jax.random.randint(jax.random.fold_in(_gk, 2), (50000,), 0, 50000, jnp.int32)
        dst = jnp.minimum((50000 * jax.random.uniform(jax.random.fold_in(_gk, 3), (50000,)) ** 2.0).astype(jnp.int32), 49999)
        _o = jnp.argsort(dst, stable=True)
        src = src[_o]
        dst = dst[_o]
        edge_attr_32 = 0.000189758 + 1.00013 * jax.random.normal(jax.random.fold_in(_gk, 12), (50000, 32), jnp.float32)
        edge_weight = jax.random.uniform(jax.random.fold_in(_gk, 14), (50000,), jnp.float32, 0.0, 0.999999)
        return (x, src, dst, edge_attr_32, edge_weight)
    x, src, dst, edge_attr_32, edge_weight = _rec_inputs()

    def _L0_gnn_setup():
        import jax, jax.numpy as jnp
        import numpy as np
        V = 3125
        E = 1250000
        C_IN = 64
        C_OUT = 64
        key = jax.random.key(seed)
        ks = jax.random.split(key, 6)
        X = jax.random.normal(ks[0], (V, C_IN), dtype=jnp.float32)
        edge_src = jax.random.randint(ks[1], (E,), 0, V, dtype=jnp.int32)
        edge_dst = jax.random.randint(ks[2], (E,), 0, V, dtype=jnp.int32)
        edge_w = jax.random.uniform(ks[3], (E,), dtype=jnp.float32)
        std = float(np.sqrt(2.0 / (C_IN + C_OUT)))
        W = jax.random.normal(ks[4], (C_IN, C_OUT), dtype=jnp.float32) * std
        b = jax.random.normal(ks[5], (C_OUT,), dtype=jnp.float32) * 0.0
        return {'X': X, 'edge_src': edge_src, 'edge_dst': edge_dst, 'edge_w': edge_w, 'W': W, 'b': b}
    _L0_gnn_all = _L0_gnn_setup()
    _L0_gnn_in = {k: v for k, v in _L0_gnn_all.items() if k in ('W', 'b')}
    del _L0_gnn_all

    def _L1_gnn_setup():
        import jax, jax.numpy as jnp
        import numpy as np
        N_NODES = 50000
        N_EDGES = 50000
        C = 64
        EDGE_H = 64
        RAW_EDGE = 32
        NUM_LAYERS = 3
        NEG_SLOPE = 0.2

        def _gatv2_layer(x, src, dst, e_proj, Wl, bl, Wr, br, att, bias, n_nodes):
            xl = x @ Wl + bl
            xr = x @ Wr + br
            e = xl[src] + xr[dst] + e_proj
            e = jnp.where(e > 0, e, NEG_SLOPE * e)
            s = e @ att
            m = jax.ops.segment_max(s, dst, num_segments=n_nodes)
            m = jnp.where(jnp.isfinite(m), m, 0.0)
            a = jnp.exp(s - m[dst])
            denom = jax.ops.segment_sum(a, dst, num_segments=n_nodes)
            alpha = a / (denom[dst] + 1e-16)
            out = jax.ops.segment_sum(xl[src] * alpha[:, None], dst, num_segments=n_nodes)
            return out + bias
        key = jax.random.key(seed)
        ks = jax.random.split(key, 16)
        inp = {'x': jax.random.normal(ks[0], (N_NODES, C), dtype=jnp.float32), 'edge_index': jax.random.randint(ks[1], (2, N_EDGES), 0, N_NODES, dtype=jnp.int64), 'edge_attr': jax.random.normal(ks[2], (N_EDGES, RAW_EDGE), dtype=jnp.float32), 'W_emb': jax.random.normal(ks[3], (RAW_EDGE, EDGE_H), dtype=jnp.float32) * RAW_EDGE ** (-0.5), 'b_emb': jnp.zeros((EDGE_H,), dtype=jnp.float32), 'Wl': jax.random.normal(ks[4], (NUM_LAYERS, C, C), dtype=jnp.float32) * C ** (-0.5), 'bl': jnp.zeros((NUM_LAYERS, C), dtype=jnp.float32), 'Wr': jax.random.normal(ks[5], (NUM_LAYERS, C, C), dtype=jnp.float32) * C ** (-0.5), 'br': jnp.zeros((NUM_LAYERS, C), dtype=jnp.float32), 'We': jax.random.normal(ks[6], (NUM_LAYERS, EDGE_H, C), dtype=jnp.float32) * EDGE_H ** (-0.5), 'att': jax.random.normal(ks[7], (NUM_LAYERS, C), dtype=jnp.float32) * C ** (-0.5), 'bias': jnp.zeros((NUM_LAYERS, C), dtype=jnp.float32)}
        return inp
    _L1_gnn_all = _L1_gnn_setup()
    _L1_gnn_in = {k: v for k, v in _L1_gnn_all.items() if k in ('W_emb', 'b_emb', 'Wl', 'bl', 'Wr', 'br', 'We', 'att', 'bias')}
    del _L1_gnn_all
    return {'x': x, 'src': src, 'dst': dst, 'edge_attr_32': edge_attr_32, 'edge_weight': edge_weight, 'L0_gnn_W': _L0_gnn_in['W'], 'L0_gnn_b': _L0_gnn_in['b'], 'L1_gnn_W_emb': _L1_gnn_in['W_emb'], 'L1_gnn_b_emb': _L1_gnn_in['b_emb'], 'L1_gnn_Wl': _L1_gnn_in['Wl'], 'L1_gnn_bl': _L1_gnn_in['bl'], 'L1_gnn_Wr': _L1_gnn_in['Wr'], 'L1_gnn_br': _L1_gnn_in['br'], 'L1_gnn_We': _L1_gnn_in['We'], 'L1_gnn_att': _L1_gnn_in['att'], 'L1_gnn_bias': _L1_gnn_in['bias']}

def reference(x, src, dst, edge_attr_32, edge_weight, L0_gnn_W, L0_gnn_b, L1_gnn_W_emb, L1_gnn_b_emb, L1_gnn_Wl, L1_gnn_bl, L1_gnn_Wr, L1_gnn_br, L1_gnn_We, L1_gnn_att, L1_gnn_bias):
    import jax
    import jax.numpy as jnp

    def _L0_gnn_ref(X, edge_src, edge_dst, edge_w, W, b):
        import jax, jax.numpy as jnp
        import numpy as np
        V = 3125
        E = 1250000
        C_IN = 64
        C_OUT = 64
        msgs = edge_w[:, None] * X[edge_src]
        f = jax.ops.segment_sum(msgs, edge_dst, num_segments=X.shape[0])
        return f @ W + b

    def _L1_gnn_ref(x, edge_index, edge_attr, W_emb, b_emb, Wl, bl, Wr, br, We, att, bias):
        import jax, jax.numpy as jnp
        import numpy as np
        N_NODES = 50000
        N_EDGES = 50000
        C = 64
        EDGE_H = 64
        RAW_EDGE = 32
        NUM_LAYERS = 3
        NEG_SLOPE = 0.2

        def _gatv2_layer(x, src, dst, e_proj, Wl, bl, Wr, br, att, bias, n_nodes):
            xl = x @ Wl + bl
            xr = x @ Wr + br
            e = xl[src] + xr[dst] + e_proj
            e = jnp.where(e > 0, e, NEG_SLOPE * e)
            s = e @ att
            m = jax.ops.segment_max(s, dst, num_segments=n_nodes)
            m = jnp.where(jnp.isfinite(m), m, 0.0)
            a = jnp.exp(s - m[dst])
            denom = jax.ops.segment_sum(a, dst, num_segments=n_nodes)
            alpha = a / (denom[dst] + 1e-16)
            out = jax.ops.segment_sum(xl[src] * alpha[:, None], dst, num_segments=n_nodes)
            return out + bias
        n = x.shape[0]
        edge_h = edge_attr @ W_emb + b_emb
        loop = jnp.arange(n, dtype=edge_index.dtype)
        src = jnp.concatenate([edge_index[0], loop])
        dst = jnp.concatenate([edge_index[1], loop])
        mean_eh = jnp.mean(edge_h, axis=0)
        edge_h_full = jnp.concatenate([edge_h, jnp.broadcast_to(mean_eh, (n, EDGE_H))], axis=0)
        h = x
        for l in range(NUM_LAYERS):
            e_proj = edge_h_full @ We[l]
            h = _gatv2_layer(h, src, dst, e_proj, Wl[l], bl[l], Wr[l], br[l], att[l], bias[l], n)
            if l < NUM_LAYERS - 1:
                h = jax.nn.relu(h)
        return h
    edge_index = jnp.stack([src, dst])
    x = _layernorm(x + _L0_gnn_ref(x, src, dst, edge_weight, L0_gnn_W, L0_gnn_b), axis=-1)
    x = _layernorm(x + _L1_gnn_ref(x, edge_index, edge_attr_32, L1_gnn_W_emb, L1_gnn_b_emb, L1_gnn_Wl, L1_gnn_bl, L1_gnn_Wr, L1_gnn_br, L1_gnn_We, L1_gnn_att, L1_gnn_bias), axis=-1)
    return x

_drawn_inputs = setup_inputs


def setup_inputs(seed=0):
    import zlib

    import numpy as np

    out = dict(_drawn_inputs(seed))
    spreads = {'L0_gnn_b': (0.0, 0.1),
     'L1_gnn_b_emb': (0.0, 0.8),
     'L1_gnn_bl': (0.0, 0.1),
     'L1_gnn_br': (0.0, 0.8),
     'L1_gnn_bias': (0.0, 0.1)}
    factors = {'L1_gnn_Wr': 3.313}
    for name, (base, spread) in spreads.items():
        noise = np.random.default_rng([zlib.crc32(name.encode()), seed]).standard_normal(out[name].shape)
        drawn = base * np.exp(spread * noise) if base else spread * noise
        out[name] = jnp.asarray(drawn.astype(out[name].dtype))
    for name, factor in factors.items():
        out[name] = (out[name] * factor).astype(out[name].dtype)
    return out
```

```python
from contextlib import ExitStack

import numpy as np
import concourse.bass as bass
from concourse import mybir

F32 = mybir.dt.float32
BF16 = mybir.dt.bfloat16
I32 = mybir.dt.int32
I16 = mybir.dt.int16
ALU = mybir.AluOpType
ACT = mybir.ActivationFunctionType
AX = mybir.AxisListType.X
ds = bass.ds

P = 128
N = 50000
E = 50000
C = 64
R = 32
GAT = 3
LAYERS = 1 + GAT
CH = 16
NCH = -(-E // (P * CH))
ET = NCH * CH
NT = ET
ROWS = ET * P
NTR = -(-N // P)
STEPS = 7
PAIRS = 2 * STEPS
ROUNDS = -(-(ET + NTR - 1) // PAIRS)
K = ROUNDS * PAIRS
W = 68
WGT, LAST, MAXI = C, C + 1, C + 2
SELP = 100
SELQ = ET // SELP
QUAD = 4
QCH = CH // QUAD
UNITS = NT // QUAD
BIG = 1e30
FAR = 1 << 17
SLOPE = 0.2
EPS = 1e-5
Y = 96
CLAMPED = "the preparation clamps the tables' values to the shapes' bounds"
PROJ = 3 * C


def w(eng, sem, value):
    if not isinstance(value, int) or value > 0:
        eng.wait_ge(sem, value)


def waits_apart(eng, reached, *waits):
    known = [(sem, v if isinstance(v, int) else eng.to_reg(v)) for sem, v in waits]
    eng.wait_ge(reached, 1)
    for sem, v in known:
        if not isinstance(v, int) or v > 0:
            eng.wait_ge(sem, v)


def chunk_loop(eng, body, layer):
    peeled = 1 if layer == 0 else 0
    body(0, 0)
    for it in range(peeled):
        for k in range(1, 5):
            body(it, k)
    with eng.Fori(peeled, (NCH - 1) // 4) as it:
        for k in range(1, 5):
            body(it, k)


def unit_loop(eng, stages):
    def turn(four, r):
        for lag, stage in stages:
            if isinstance(four, int) and not 0 <= 4 * four + r - lag < UNITS:
                continue
            stage(4 * four + (r - lag), (r - lag) % 4, four + (r - lag) // 4 + 1)
    lags = max(lag for lag, _ in stages)
    peeled = -(-lags // 4) + 1
    for x in range(peeled):
        for r in range(4):
            turn(x, r)
    with eng.Fori(peeled, UNITS // 4) as it:
        for r in range(4):
            turn(it, r)
    for r in range(lags):
        turn(UNITS // 4 + r // 4, r % 4)


def build(nc, io):
    ctx = ExitStack()
    with ctx:
        def sb(name, shape, dt=F32):
            return ctx.enter_context(nc.sbuf_tensor(name, shape, dt))

        def sem(name):
            return ctx.enter_context(nc.semaphore(name))

        def dram(name, shape, dt=F32):
            return nc.dram_tensor(name, shape, dt, kind="Internal").ap()

        xl_tab = [dram(f"xl_tab{i}", (ROWS, C)) for i in range(2)]
        xr_tab = [dram(f"xr_tab{i}", (ROWS, C)) for i in range(2)]
        x1_tab = dram("x1_tab", (ROWS, C))

        def unit_rows(tab, u):
            return tab.rearrange("(t p) c -> p t c", p=P)[:, ds(QUAD * u, QUAD), :]

        nodes = sb("nodes", [P, NT, W])
        msg = sb("msg", [P, 4 * CH, W])
        dst_rel = sb("dst_rel", [P, K + PAIRS])
        same_prev = sb("same_prev", [CH, NCH, P], BF16)
        same_next = sb("same_next", [CH, NCH, P], BF16)
        edge_idx = sb("edge_idx", [P, 4, 2, CH], I32)
        last_edge = sb("last_edge", [P, ET], BF16)
        crosses = sb("crosses", [P, ET], BF16)
        cross_ring = sb("cross_ring", [P, 2, CH])
        row_f = sb("row_f", [1, ET])
        row_b = sb("row_b", [1, ET])
        goes_on = sb("goes_on", [1, NCH])
        pair_tab = sb("pair_tab", [1, ROUNDS, 4, 8], I16)
        tile_tab = sb("tile_tab", [1, ROUNDS, 4], I32)
        round_tab = sb("round_tab", [1, 32], I32)
        hot = [sb(f"hot{i}", [P, STEPS, P]) for i in range(2)]
        ident = sb("ident", [P, P])
        iota_f = sb("iota_f", [P, P])
        part_id = sb("part_id", [P, 1])
        zero_row = sb("zero_row", [P, W])
        zeros_b = sb("zeros_b", [1, 512], BF16)
        we = sb("we", [R + 1, GAT, C])
        pw = sb("pw", [C + 1, GAT, PROJ])
        w0 = sb("w0", [C + 1, Y])
        att_b = sb("att_b", [P, GAT, C])
        bias_c = sb("bias_c", [C, GAT])
        bias_b = sb("bias_b", [P, C])
        self_score = sb("self_score", [P, NT])
        c_edge = sb("c_edge", [P, NT])
        weight = c_edge
        c_self = sb("c_self", [P, NT])
        score = sb("score", [P, 2, CH])
        scan_f = sb("scan_f", [CH, P])
        scan_b = sb("scan_b", [CH, P])
        seg_max = sb("seg_max", [CH, P])
        fwd_row = sb("fwd_row", [1, 2, CH + 1])
        bwd_row = sb("bwd_row", [1, CH + 1])
        neg_arg = sb("neg_arg", [1, 1])
        rescale = sb("rescale", [1, 1])
        less_max = sb("less_max", [P, CH])
        init = sb("init", [CH, 2])
        eps_c = sb("eps_c", [P, 1])
        relu_z = sb("relu_z", [P, 2, QUAD, C])
        leaky = sb("leaky", [P, 2, QUAD, C])
        weighted = sb("weighted", [P, 2, QUAD, C])
        stat = sb("stat", [P, 4, 4, QUAD])

        region = sb("region", [P, 8192])

        def part(at, n, shape, rows=P):
            v = region[0:rows, at:at + n]
            names = " ".join("abcd"[:len(shape)])
            return v.rearrange(f"p ({names}) -> p {names}", **dict(zip("abcd", shape)))

        gathered = part(0, 2048, (2, CH, C))
        gathered_r = part(2048, 2048, (2, CH, C))
        attr = part(4096, 2048, (4, 512), R + 1)
        h = part(0, 1024, (4, QUAD, C))
        t_self = part(1024, 1024, (4, QUAD, C))
        loaded = part(2048, 1024, (4, QUAD, C))
        projected = part(3072, 3072, (4, QUAD, PROJ))
        h_t = part(6144, 2048, (4, 512), C + 1)
        sums = msg[:, :, :].rearrange("p t w -> p (t w)")[:, 0:2 * QUAD * C].rearrange(
            "p (s t c) -> p s t c", s=2, t=QUAD)
        centered = [t_self, part(6144, 1024, (4, QUAD, C))]
        normed = [h, part(7168, 1024, (4, QUAD, C))]

        bank = [ctx.enter_context(nc.psum_tensor(f"bank{i}", [P, 512], F32)) for i in range(8)]
        z_ps = bank[0:2]
        tr_ps = bank[2]
        row_ps = bank[3]
        win_ps = bank[4:6]
        carry_ps = bank[6]
        ht_ps = bank[0:2]
        y_ps = bank[2:4]
        pj_ps = bank[4:8]

        loads = sem("loads")
        consts = sem("consts")
        prep_v = sem("prep_v")
        prep_t = sem("prep_t")

        scratch = nodes[:, :, :].rearrange("p t w -> p (t w)")
        spare = msg[:, :, :].rearrange("p t w -> p (t w)")
        at = [0]

        def temp(shape, dt=F32, rows=P, place=None):
            n = int(np.prod(shape))
            words = n if dt in (F32, I32) else -(-n // 2)
            if place is None:
                v = scratch[0:rows, at[0]:at[0] + words]
                at[0] += words
            else:
                v = place[0:rows, 0:words]
            if dt is not F32:
                v = v.bitcast(dt)
            if len(shape) > 1:
                names = " ".join("abcd"[:len(shape)])
                v = v.rearrange(f"p ({names}) -> p {names}", **dict(zip("abcd", shape)))
            return v

        HALF = E // 8
        last_i = temp((SELQ,), I32, SELP)
        rows_i = temp((3, SELQ, P), I32, SELP, region[:, HALF:HALF + 3 * SELQ * P])
        drow = temp((SELQ, P), F32, SELP)
        drow2 = temp((SELQ, P), F32, SELP)
        cols_i = temp((4, ET), I32)
        ccol = temp((2, ET))
        win_i = temp((NCH, P + 2), I32, CH)
        win_f = temp((NCH, P + 1), F32, CH)
        ends_i = temp((2, ET + 1), I32, 1)
        ends_f = temp((ET,), F32, 1)
        chunk_i = temp((3, NCH), I32, 1)
        chunk_f = temp((NCH,), F32, 1)
        round_i = temp((NCH, ROUNDS), I32, 1, spare)
        round_c = temp((NCH, ROUNDS), F32, 1, spare[:, NCH * ROUNDS:])
        round_f = temp((NCH,), F32, 1)
        tile_i = temp((SELQ,), I32)
        tile_f = temp((SELQ,))
        v_f = temp((SELQ,), F32, SELP)
        k_i = temp((K,), I32)
        k_f = temp((K,))
        ik_f = temp((K,))
        jk_f = temp((K,))
        before = temp((SELQ, K), BF16, SELP)
        pick = temp((SELQ, K), F32, SELP)
        ones_b = temp((P,), BF16, SELP)
        ring_i = temp((K,), I32, 1)
        chunk_k = temp((NCH,), I32, 1)
        iota_i = temp((P,), I32)
        pid_i = temp((1,), I32)
        attr_a = temp((HALF,), F32, P, region)
        attr_b = temp((HALF,))
        attr_sum = temp((1,))
        attr_sum2 = temp((1,))
        fold = temp((R,))
        mean_c = temp((C + 1,), F32, R + 1)
        emb_t = temp((R + 1,), F32, C)
        we_in = temp((GAT, C), F32, C)
        assert at[0] <= NT * W
        HK = K // 2

        N_LOADS = 28

        idx_in = [sem(f"idx_in{i}") for i in range(4)]
        gat_in = [sem(f"gat_in{i}") for i in range(8)]
        attr_in = [sem(f"attr_in{i}") for i in range(4)]
        z_done = sem("z_done")
        relu_done = sem("relu_done")
        leaky_done = sem("leaky_done")
        att_done = sem("att_done")
        score_done = sem("score_done")
        score_t = sem("score_t")
        scans = sem("scans")
        ends_t = sem("ends_t")
        rows_done = sem("rows_done")
        rows_t = sem("rows_t")
        init_done = sem("init_done")
        scans2 = sem("scans2")
        max_done = sem("max_done")
        arg_done = sem("arg_done")
        max_t = sem("max_t")
        less_done = sem("less_done")
        flags_done = sem("flags_done")
        rescale_done = sem("rescale_done")
        exp_done = sem("exp_done")
        msg_done = sem("msg_done")
        cross_done = sem("cross_done")
        carried = sem("carried")
        carry_done = sem("carry_done")
        hot_done = [sem(f"hot_done{i}") for i in range(2)]
        win_done = [sem(f"win_done{i}") for i in range(2)]
        add_done = [sem(f"add_done{i}") for i in range(2)]

        row_in = [sem(f"row_in{i}") for i in range(4)]
        res_in = [sem(f"res_in{i}") for i in range(4)]
        row_out = [sem(f"row_out{i}") for i in range(4)]
        norm_out = [sem(f"norm_out{i}") for i in range(4)]
        copy_done = sem("copy_done")
        f_t = sem("f_t")
        f_t_copied = sem("f_t_copied")
        y_done = sem("y_done")
        mean_sum = sem("mean_sum")
        mean_done = sem("mean_done")
        center_done = sem("center_done")
        square_done = sem("square_done")
        var_done = sem("var_done")
        dev_done = sem("dev_done")
        inv_done = sem("inv_done")
        norm_done = sem("norm_done")
        coef_v = sem("coef_v")
        coef_a = sem("coef_a")
        edge_part = sem("edge_part")
        self_part = sem("self_part")
        cleared = sem("cleared")
        h_done = sem("h_done")
        h_t_done = sem("h_t_done")
        h_t_copied = sem("h_t_copied")
        proj_done = sem("proj_done")
        proj_copied = sem("proj_copied")
        s_leaky = sem("s_leaky")
        s_att = sem("s_att")
        s_score = sem("s_score")
        res_added = sem("res_added")

        EVEN = [(NCH + 1) // 2, NCH // 2]

        def gath_target(layer, it, k, q):
            kk = k + NCH * layer
            uses = 2 * it + kk // 2 + 1
            if layer == 0:
                return uses * 16 * QUAD
            return 16 * QUAD * EVEN[kk % 2] + (uses - EVEN[kk % 2]) * 32 * QUAD

        block = ctx.enter_context(nc.Block())

        @block.sync
        def _(sp):
            def load(to, frm):
                sp.dma_start(to, frm).then_inc(loads, 16)

            load(last_i, io["tile_last"])
            load(rows_i[:, 0], io["row_dst"].rearrange("(q p) l -> p q l", p=SELP))
            load(rows_i[:, 1], io["row_clast"].rearrange("(q p) l -> p q l", p=SELP))
            load(rows_i[:, 2], io["row_cnext"].rearrange("(q p) l -> p q l", p=SELP))
            load(cols_i, io["col_ids"].rearrange("a p t -> p a t"))
            load(win_i, io["win_dst"])
            load(ends_i, io["row_ends"])
            load(chunk_i, io["chunk_ends"])
            load(weight[:, :], io["col_weight"])
            for s in range(4):
                load(attr_a[s * R:(s + 1) * R], io["attr_t"][0:R, 2 * s * HALF:(2 * s + 1) * HALF])
                load(attr_b[s * R:(s + 1) * R], io["attr_t"][0:R, (2 * s + 1) * HALF:(2 * s + 2) * HALF])
            load(emb_t, io["emb_t"])
            load(we_in, io["We"].rearrange("l k c -> k l c"))
            load(pw[0:C, :, 0:C], io["Wl"].rearrange("l k c -> k l c"))
            load(pw[0:C, :, C:2 * C], io["Wr"].rearrange("l k c -> k l c"))
            load(pw[C:C + 1, :, 0:C], io["bl"][None])
            load(pw[C:C + 1, :, C:2 * C], io["br"][None])
            load(w0[0:C, 0:C], io["W0"])
            load(w0[C:C + 1, 0:C], io["b0"][None])
            load(att_b[:, :, :], io["att"][None].to_broadcast([P, GAT, C]))
            load(bias_c[:, :], io["bias_t"])
            load(bias_b[:, :], io["bias"][GAT - 1:GAT, :].to_broadcast([P, C]))

            def edge_phase(layer):
                def idx(it, k):
                    kk = k + NCH * layer
                    w(sp, msg_done, 4 * it + kk - 3)
                    sp.dma_start(edge_idx[:, kk % 4], io["edge_idx"][ds(4 * it + k, 1)].rearrange(
                        "o p a t -> (o p) a t")).then_inc(idx_in[kk % 4], 16)

                def body(it, k):
                    idx(it, k)
                    if layer == 0:
                        return
                    for q in range(QCH):
                        n = 4 * (4 * it + k + NCH * (layer - 1)) + q
                        w(sp, z_done, n - 3)
                        sp.dma_start(attr[:, q, :], io["attr_t"][:, ds((4 * it + k) * CH * P + q * 512, 512)]
                                     ).then_inc(attr_in[q], 16)
                if layer:
                    for s in range(4):
                        sp.wait_ge(row_out[s], PER_LAYER * layer)
                        sp.wait_ge(norm_out[s], PER_LAYER // 2)
                    sp.wait_ge(s_score, UNITS * layer)
                chunk_loop(sp, body, layer)

            def node_phase(layer):
                n0 = UNITS * layer
                cur = (layer - 1) % 2
                nxt = layer % 2

                def fetch(u, s, n):
                    if layer == 0:
                        w(sp, y_done, u - 3)
                        sp.dma_start(loaded[:, s], unit_rows(io["x"], u)).then_inc(row_in[s], 16)
                    else:
                        w(sp, self_part, UNITS * (layer - 1) + u - 3)
                        sp.dma_start(loaded[:, s], unit_rows(xl_tab[cur], u)).then_inc(row_in[s], 16)
                    if layer == GAT:
                        sp.dma_start(projected[:, s, :, 0:C], unit_rows(x1_tab, u)).then_inc(res_in[s], 16)

                def store_norm(u, s, n):
                    sp.wait_ge(norm_done, (0 if layer == 0 else UNITS) + u + 1)
                    to = x1_tab if layer == 0 else io["out"]
                    sp.dma_start(unit_rows(to, u), normed[layer // GAT][:, s]).then_inc(norm_out[s], 16)

                def store_proj(u, s, n):
                    sp.wait_ge(proj_copied, 2 * (n0 + u + 1))
                    sp.dma_start(unit_rows(xl_tab[nxt], u), projected[:, s, :, 0:C]).then_inc(row_out[s], 16)
                    sp.dma_start(unit_rows(xr_tab[nxt], u), projected[:, s, :, C:2 * C]).then_inc(row_out[s], 16)

                sp.wait_ge(add_done[1], ROUNDS * (layer + 1) + 1)
                if layer == 0:
                    unit_loop(sp, [(0, fetch), (9, store_norm), (13, store_proj)])
                elif layer < GAT:
                    unit_loop(sp, [(0, fetch), (8, store_proj)])
                else:
                    unit_loop(sp, [(0, fetch), (9, store_norm)])

            for layer in range(LAYERS):
                edge_phase(layer)
                node_phase(layer)
            for s in range(4):
                sp.wait_ge(norm_out[s], PER_LAYER)

        @block.gpsimd
        def _(pool):
            g = nc.gpsimd
            g.memset(ident[:, :], 0.0).then_inc(consts, 1)
            g.memset(zeros_b[:, :], 0.0).then_inc(consts, 1)
            g.memset(zero_row[:, :], 0.0).then_inc(consts, 1)
            g.memset(ones_b, 1.0).then_inc(consts, 1)
            g.memset(mean_c, 0.0).then_inc(consts, 1)
            g.iota(iota_i, pattern=[[1, P]], base=0, channel_multiplier=0).then_inc(consts, 1)
            g.iota(pid_i, pattern=[[0, 1]], base=0, channel_multiplier=1).then_inc(consts, 1)
            g.iota(tile_i, pattern=[[SELP, SELQ]], base=0, channel_multiplier=1).then_inc(consts, 1)
            g.iota(chunk_k, pattern=[[CH, NCH]], base=CH, channel_multiplier=0).then_inc(consts, 1)
            g.iota(round_i, pattern=[[0, NCH], [PAIRS, ROUNDS]], base=PAIRS,
                   channel_multiplier=0).then_inc(consts, 1)
            g.iota(k_i, pattern=[[1, K]], base=0, channel_multiplier=0).then_inc(consts, 1)
            pool.wait_ge(consts, 11)
            g.affine_select(out=ident[:, :], in_=ident[:, :], compare_op=ALU.not_equal, fill=1.0,
                            base=0, pattern=[[-1, P]], channel_multiplier=1).then_inc(consts, 1)
            pool.wait_ge(consts, 12)
            g.memset(mean_c[R:R + 1, C:C + 1], 1.0).then_inc(consts, 1)

            pool.wait_ge(prep_v, PV["all"])

            def edge_phase(layer):
                table = io["x"] if layer == 0 else xl_tab[(layer - 1) % 2]

                def body(it, k):
                    kk = k + NCH * layer
                    waits_apart(pool, consts, (idx_in[kk % 4], 16 * (it + kk // 4 + 1)),
                                (msg_done, 4 * it + kk - 1))
                    for t in range(CH):
                        q = (kk % 2) * QCH + t // QUAD
                        pool.indirect_dma_start(
                            gathered[:, kk % 2, t, :], None, table,
                            bass.IndirectOffsetOnAxis(edge_idx[:, kk % 4, 0, t:t + 1], 0),
                        ).then_inc(gat_in[q], 16)
                        if layer:
                            pool.indirect_dma_start(
                                gathered_r[:, kk % 2, t, :], None, xr_tab[(layer - 1) % 2],
                                bass.IndirectOffsetOnAxis(edge_idx[:, kk % 4, 1, t:t + 1], 0),
                            ).then_inc(gat_in[q], 16)
                if layer:
                    for s in range(4):
                        pool.wait_ge(row_out[s], PER_LAYER * layer)
                        pool.wait_ge(norm_out[s], PER_LAYER // 2)
                    pool.wait_ge(s_score, UNITS * layer)
                chunk_loop(pool, body, layer)

            def node_phase(layer):
                n0 = UNITS * (layer - 1)

                def clear(u, s, n):
                    if layer == 0:
                        pool.wait_ge(copy_done, u + 1)
                    else:
                        pool.wait_ge(edge_part, n0 + u + 1)
                    g.tensor_copy(nodes[:, ds(QUAD * u, QUAD), :],
                                  zero_row[:, None, :].to_broadcast([P, QUAD, W])).then_inc(cleared, 1)

                def self_share(u, s, n):
                    pool.wait_ge(row_in[s], 16 * ((UNITS // 4) * layer + n))
                    w(pool, h_done, n0 + u - 3)
                    ins = g.tensor_tensor(t_self[:, s], loaded[:, s],
                                          c_self[:, ds(QUAD * u, QUAD)][:, :, None].to_broadcast([P, QUAD, C]),
                                          ALU.mult)
                    if layer < GAT:
                        ins.then_inc(self_part, 1)
                        return
                    ins.then_inc(res_added, 1)
                    res = projected[:, s, :, 0:C]
                    pool.wait_ge(res_in[s], 16 * n)
                    g.tensor_tensor(res, res, bias_b[:, None, :].to_broadcast([P, QUAD, C]),
                                    ALU.add).then_inc(res_added, 1)
                    pool.wait_ge(res_added, 2 * (u + 1))
                    g.tensor_tensor(t_self[:, s], t_self[:, s], res, ALU.add).then_inc(self_part, 1)

                if layer == 0:
                    unit_loop(pool, [(1, clear)])
                else:
                    pool.wait_ge(coef_v, 10 * layer)
                    unit_loop(pool, [(2, self_share)] + ([(3, clear)] if layer < GAT else []))

            for layer in range(LAYERS):
                edge_phase(layer)
                node_phase(layer)

        @block.tensor
        def _(pe):
            mm, tr = nc.tensor.matmul, nc.tensor.transpose
            pe.wait_ge(prep_v, PV["before"])
            for half in range(2):
                for q in range(SELQ):
                    last = mm(bank[half][:, 0:HK], ones_b[:, :], before[:, q, half * HK:(half + 1) * HK],
                              start=q == 0, stop=q == SELQ - 1)
            last.then_inc(prep_t, 1)
            pe.wait_ge(prep_v, PV["pick"])
            for half in range(2):
                for q in range(SELQ):
                    last = mm(bank[2 + half][:, 0:HK], drow[:, q, :], pick[:, q, half * HK:(half + 1) * HK],
                              start=q == 0, stop=q == SELQ - 1)
            last.then_inc(prep_t, 1)
            pe.wait_ge(prep_v, PV["fold"])
            mm(bank[4][0:R, 0:1], fold, attr_sum, start=True, stop=True)
            for n in range(GAT):
                last = mm(bank[5][0:R + 1, n * C:(n + 1) * C], emb_t, we_in[:, n, :], start=True, stop=True)
            last.then_inc(prep_t, 1)
            pe.wait_ge(prep_v, PV["we"])
            for n in range(GAT):
                last = mm(bank[6][0:C + 1, n * C:(n + 1) * C], mean_c, we[:, n, :], start=True, stop=True)
            last.then_inc(prep_t, 1)

            def rounds(layer, c):
                lo = pe.value_load(round_tab[0:1, ds(c, 1)], min_val=0, max_val=ROUNDS)
                hi = pe.value_load(round_tab[0:1, ds(c + 1, 1)], min_val=0, max_val=ROUNDS)
                with pe.Fori(lo, hi) as r:
                    g = r + (ROUNDS * layer + 1)
                    for b in range(2):
                        _, ring = nc.values_load_multi_w_load_instructions(
                            pair_tab[0:1, ds(r, 1), b, 0:STEPS].rearrange("p a b -> p (a b)"),
                            engines=(PE,), min_val=0, max_val=4 * CH - 1,
                            skip_runtime_bounds_check_because=CLAMPED)
                        _, off = nc.values_load_multi_w_load_instructions(
                            pair_tab[0:1, ds(r, 1), 2 + b, 0:STEPS].rearrange("p a b -> p (a b)"),
                            engines=(PE,), min_val=0, max_val=STEPS - 1,
                            skip_runtime_bounds_check_because=CLAMPED)
                        pe.wait_ge(add_done[b], g)
                        mm(win_ps[b][:, 0:STEPS * W], zeros_b[:, 0:P], zeros_b[:, 0:STEPS * W],
                           start=True, stop=True, skip_group_check=True)
                        pe.wait_ge(hot_done[b], g + 1)
                        for s in range(STEPS):
                            last = mm(win_ps[b][:, ds(off[s] * W, W)], hot[b][:, s, :],
                                      msg[:, ds(ring[s], 1), :].rearrange("p o w -> p (o w)"),
                                      start=False, stop=True, skip_group_check=True)
                        last.then_inc(win_done[b], 1)

            def carry(layer, it, k):
                kk = k + NCH * layer
                n = 4 * it + kk
                if isinstance(it, int) and k == 0:
                    pe.wait_ge(msg_done, n + 1)
                w(pe, carried, 4 * it + k + (NCH - 1) * layer)
                pe.wait_ge(cross_done, n + 1)
                for t in range(CH):
                    last = mm(carry_ps[0:1, 0:W], cross_ring[:, kk % 2, t:t + 1],
                              msg[:, (k % 4) * CH + t, :], start=t == 0, stop=t == CH - 1)
                last.then_inc(carry_done, 1)

            def edge_phase(layer):
                def scores(it, k):
                    kk = k + NCH * layer
                    n1 = 4 * it + k + NCH * (layer - 1)
                    for q in range(QCH):
                        nq = 4 * n1 + q
                        slot = kk % 2 * QCH + q
                        pe.wait_ge(gat_in[slot], gath_target(layer, it, k, q))
                        pe.wait_ge(attr_in[q], 16 * (n1 + 1))
                        w(pe, leaky_done, nq - 1)
                        z = z_ps[q % 2]
                        rows = slice(q * QUAD, (q + 1) * QUAD)
                        mm(z[:, 0:QUAD * C], ident[:, :], gathered[:, kk % 2, rows, :].rearrange("p a b -> p (a b)"),
                           start=True, stop=True, skip_group_check=True)
                        mm(z[:, 0:QUAD * C], ident[:, :], gathered_r[:, kk % 2, rows, :].rearrange("p a b -> p (a b)"),
                           start=False, stop=True, skip_group_check=True)
                        for t in range(QUAD):
                            last = mm(z[:, t * C:(t + 1) * C], attr[:, q, t * P:(t + 1) * P],
                                      we[:, layer - 1, :], start=False, stop=t == QUAD - 1,
                                      skip_group_check=True)
                        last.then_inc(z_done, 1)
                    waits_apart(pe, consts, (score_done, QCH * (n1 + 1)))
                    tr(tr_ps[0:CH, 0:P], score[:, kk % 2, :], ident[:, :]).then_inc(score_t, 1)
                    waits_apart(pe, consts, (scans, 2 * (n1 + 1)))
                    tr(row_ps[0:1, 0:CH], scan_f[:, P - 1:P], ident[0:CH, 0:CH])
                    tr(row_ps[0:1, CH:2 * CH], scan_b[:, 0:1], ident[0:CH, 0:CH]).then_inc(ends_t, 1)
                    waits_apart(pe, consts, (rows_done, 3 * (n1 + 1)))
                    tr(row_ps[0:CH, 32:33], fwd_row[:, kk % 2, 0:CH], ident[0:1, 0:1])
                    tr(row_ps[0:CH, 33:34], bwd_row[:, 1:CH + 1], ident[0:1, 0:1]).then_inc(rows_t, 1)
                    waits_apart(pe, consts, (max_done, n1 + 1))
                    tr(row_ps[:, 64:64 + CH], seg_max[:, :], ident[0:CH, 0:CH]).then_inc(max_t, 1)

                def body(it, k):
                    if layer:
                        scores(it, k)
                    if not (isinstance(it, int) and k == 0):
                        rounds(layer, 4 * it + k - 1)
                    carry(layer, it, k)

                if layer:
                    pe.wait_ge(proj_copied, 2 * UNITS * layer)
                chunk_loop(pe, body, layer)
                rounds(layer, NCH - 1)

            def node_phase(layer):
                n0 = UNITS * layer

                def f_transpose(u, s, n):
                    waits_apart(pe, consts, (copy_done, u + 1), (f_t_copied, u))
                    for t in range(QUAD):
                        last = tr(ht_ps[0][0:C, t * P:(t + 1) * P], sums[:, s % 2, t, :], ident[:, :])
                    last.then_inc(f_t, 1)

                def y(u, s, n):
                    pe.wait_ge(f_t_copied, u + 1)
                    pe.wait_ge(row_in[s], 16 * n)
                    w(pe, center_done, u - 1)
                    for t in range(QUAD):
                        mm(y_ps[s % 2][:, t * Y:(t + 1) * Y], h_t[:, s % 2, t * P:(t + 1) * P], w0[:, :],
                           start=t == 0, stop=True, skip_group_check=True)
                    mm(y_ps[s % 2][:, 0:QUAD * Y].rearrange("p (t c) -> p t c", t=QUAD)[:, :, 0:C],
                       ident[:, :], loaded[:, s], start=False, stop=True,
                       skip_group_check=True).then_inc(y_done, 1)

                def h_transpose(u, s, n):
                    if layer == 0:
                        waits_apart(pe, consts, (norm_done, u + 1), (h_t_copied, u))
                    else:
                        waits_apart(pe, consts, (h_done, n0 - UNITS + u + 1), (h_t_copied, n0 + u - 1))
                    for t in range(QUAD):
                        last = tr(ht_ps[1 if layer == 0 else s % 2][0:C, t * P:(t + 1) * P], h[:, s, t, :],
                                  ident[:, :])
                    last.then_inc(h_t_done, 1)

                def project(u, s, n):
                    pe.wait_ge(h_t_copied, n0 + u + 1)
                    w(pe, proj_copied, 2 * (n0 + u - 1))
                    for t in range(QUAD):
                        last = mm(pj_ps[2 * (s % 2) + t // 2][:, t % 2 * PROJ:(t % 2 + 1) * PROJ],
                                  h_t[:, 2 + s % 2, t * P:(t + 1) * P], pw[:, layer, :],
                                  start=t % 2 == 0, stop=t % 2 == 1, skip_group_check=True)
                    last.then_inc(proj_done, 1)

                pe.wait_ge(add_done[1], ROUNDS * (layer + 1) + 1)
                if layer == 0:
                    unit_loop(pe, [(3, y), (11, project), (1, f_transpose), (9, h_transpose)])
                elif layer < GAT:
                    unit_loop(pe, [(6, project), (4, h_transpose)])

            for layer in range(LAYERS):
                edge_phase(layer)
                node_phase(layer)

        @block.scalar
        def _(act):
            a = nc.scalar.activation
            act.wait_ge(prep_v, PV["all"])

            def edge_phase(layer):
                def body(it, k):
                    kk = k + NCH * layer
                    n = 4 * it + kk
                    n1 = n - NCH
                    ring = (k % 4) * CH
                    if layer:
                        for q in range(QCH):
                            nq = 4 * n1 + q
                            act.wait_ge(z_done, nq + 1)
                            w(act, leaky_done, nq - 1)
                            a(relu_z[:, q % 2], z_ps[q % 2][:, 0:QUAD * C].rearrange("p (t c) -> p t c", t=QUAD),
                              ACT.Relu, scale=1.0 - SLOPE).then_inc(relu_done, 1)
                        act.wait_ge(arg_done, n1 + 1)
                        w(act, carried, 4 * it + k - 1 + (NCH - 1) * layer)
                        a(rescale[:, :], neg_arg[:, :], ACT.Exp, scale=-1.0).then_inc(rescale_done, 1)
                        act.wait_ge(less_done, n1 + 1)
                        w(act, carry_done, n - 1)
                        a(msg[:, ring:ring + CH, WGT], less_max[:, :], ACT.Exp).then_inc(exp_done, 1)
                        act.wait_ge(exp_done, n1 + 1)
                        for t in range(CH):
                            last = a(msg[:, ring + t, 0:C], gathered[:, kk % 2, t, :], ACT.Copy,
                                     scale=msg[:, ring + t, WGT:WGT + 1])
                    else:
                        w(act, carry_done, n - 1)
                        for t in range(CH):
                            if t % QUAD == 0:
                                act.wait_ge(gat_in[kk % 2 * QCH + t // QUAD],
                                            gath_target(0, it, k, t // QUAD))
                            last = a(msg[:, ring + t, 0:C], gathered[:, kk % 2, t, :], ACT.Copy,
                                     scale=weight[:, ds((4 * it + k) * CH + t, 1)])
                    last.then_inc(msg_done, 1)

                if layer:
                    act.wait_ge(win_done[1], ROUNDS * layer + 1)
                chunk_loop(act, body, layer)

            def node_phase(layer):
                n0 = UNITS * layer
                ln0 = 0 if layer == 0 else UNITS

                def copy_sums(u, s, n):
                    w(act, f_t, u - 1)
                    a(sums[:, s % 2], nodes[:, ds(QUAD * u, QUAD), 0:C], ACT.Copy).then_inc(copy_done, 1)

                def f_copy(u, s, n):
                    act.wait_ge(f_t, u + 1)
                    w(act, y_done, u - 1)
                    a(h_t[0:C, s % 2, :], ht_ps[0][0:C, :], ACT.Copy).then_inc(f_t_copied, 1)

                def square(u, s, n):
                    act.wait_ge(center_done, ln0 + u + 1)
                    w(act, var_done, ln0 + u - 1)
                    a(leaky[:, s % 2], centered[layer // GAT][:, s], ACT.Square).then_inc(square_done, 1)

                def deviation(u, s, n):
                    act.wait_ge(var_done, ln0 + u + 1)
                    a(stat[:, s, 2], stat[:, s, 1], ACT.Sqrt, bias=eps_c[:, 0:1], scale=1.0 / C).then_inc(dev_done, 1)

                def h_copy(u, s, n):
                    act.wait_ge(h_t_done, n0 + u + 1)
                    w(act, proj_done, n0 + u - 1)
                    if layer:
                        a(h_t[0:C, 2 + s % 2, :], ht_ps[s % 2][0:C, :], ACT.Relu,
                          bias=bias_c[:, layer - 1:layer]).then_inc(h_t_copied, 1)
                    else:
                        a(h_t[0:C, 2 + s % 2, :], ht_ps[1][0:C, :], ACT.Copy).then_inc(h_t_copied, 1)

                def proj_copy(u, s, n):
                    act.wait_ge(proj_done, n0 + u + 1)
                    w(act, s_leaky, n0 + u - 3)
                    w(act, row_out[s], PER_LAYER * layer + 32 * (n - 1))
                    for b in range(2):
                        a(projected[:, s, 2 * b:2 * b + 2, :],
                          pj_ps[2 * (s % 2) + b][:, 0:2 * PROJ].rearrange("p (t c) -> p t c", t=2),
                          ACT.Copy).then_inc(proj_copied, 1)

                if layer:
                    act.wait_ge(coef_v, 10 * (layer - 1) + 4)
                    a(c_edge[:, :], c_edge[:, :], ACT.Exp).then_inc(coef_a, 1)
                    a(c_self[:, :], c_self[:, :], ACT.Exp).then_inc(coef_a, 1)
                else:
                    act.wait_ge(add_done[1], ROUNDS + 1)
                    act.wait_ge(msg_done, NCH)
                if layer == 0:
                    unit_loop(act, [(2, f_copy), (10, h_copy), (5, square), (7, deviation),
                                    (12, proj_copy), (0, copy_sums)])
                elif layer < GAT:
                    unit_loop(act, [(5, h_copy), (7, proj_copy)])
                else:
                    unit_loop(act, [(7, deviation), (5, square)])

            for layer in range(LAYERS):
                edge_phase(layer)
                node_phase(layer)

        @block.vector
        def _(dve):
            v = nc.vector
            step = [0]

            def seq(ins):
                step[0] += 1
                ins.then_inc(prep_v, 1)
                dve.wait_ge(prep_v, step[0])

            dve.wait_ge(loads, 16 * N_LOADS)
            dve.wait_ge(consts, 13)
            seq(v.tensor_copy(iota_f[:, :], iota_i))
            seq(v.tensor_copy(part_id[:, :], pid_i))
            seq(v.tensor_copy(k_f, k_i))
            seq(v.tensor_copy(tile_f, tile_i))
            seq(v.tensor_scalar(last_i, last_i, 7, None, ALU.logical_shift_right))
            seq(v.tensor_copy(v_f, last_i))
            seq(v.tensor_scalar(v_f, v_f, float(NTR - 1), None, ALU.min))
            seq(v.tensor_tensor(v_f, v_f, tile_f[0:SELP], ALU.add))
            for q in range(SELQ):
                seq(v.tensor_scalar(before[:, q, :], k_f[0:SELP], v_f[:, q:q + 1], None, ALU.is_gt))
            assert step[0] == PV["before"]
            seq(v.tensor_tensor(drow, rows_i[:, 0], rows_i[:, 1], ALU.is_equal))
            seq(v.tensor_tensor(drow2, rows_i[:, 1], rows_i[:, 2], ALU.is_equal))
            seq(v.tensor_tensor(drow, drow, drow2, ALU.mult))
            seq(v.tensor_scalar(drow, drow, float(FAR), None, ALU.mult))
            seq(v.tensor_tensor(drow, drow, rows_i[:, 0], ALU.add))
            dve.wait_ge(prep_t, 1)
            for half in range(2):
                seq(v.tensor_scalar(ik_f[:, half * HK:(half + 1) * HK], bank[half][:, 0:HK],
                                    float(ET - 1), None, ALU.min))
            for q in range(SELQ):
                seq(v.tensor_scalar(pick[:, q, :], ik_f[0:SELP], tile_f[0:SELP, q:q + 1], None, ALU.is_equal))
            assert step[0] == PV["pick"]
            seq(v.tensor_tensor(jk_f, k_f, ik_f, ALU.subtract))
            seq(v.tensor_scalar(jk_f, jk_f, float(NTR - 1), None, ALU.min))
            seq(v.tensor_reduce(attr_sum, attr_a, AX, ALU.add))
            seq(v.tensor_reduce(attr_sum2, attr_b, AX, ALU.add))
            seq(v.tensor_tensor(attr_sum, attr_sum, attr_sum2, ALU.add))
            seq(v.tensor_tensor(fold, ident[:, 0:R], ident[:, R:2 * R], ALU.add))
            seq(v.tensor_tensor(fold, fold, ident[:, 2 * R:3 * R], ALU.add))
            seq(v.tensor_tensor(fold, fold, ident[:, 3 * R:4 * R], ALU.add))
            assert step[0] == PV["fold"]
            dve.wait_ge(prep_t, 3)
            seq(v.tensor_scalar(mean_c[0:R, C:C + 1], bank[4][0:R, 0:1], 1.0 / E, None, ALU.mult))
            seq(v.tensor_copy(we[:, :, :].rearrange("p a b -> p (a b)"), bank[5][0:R + 1, 0:GAT * C]))
            assert step[0] == PV["we"]
            for half in range(2):
                sl = slice(half * HK, (half + 1) * HK)
                seq(v.scalar_tensor_tensor(out=dst_rel[:, sl], in0=jk_f[:, sl], scalar=float(-P),
                                           in1=bank[2 + half][:, 0:HK], op0=ALU.mult, op1=ALU.add))
            seq(v.tensor_copy(dst_rel[:, K:], dst_rel[:, 0:PAIRS]))
            seq(v.tensor_copy(ring_i, ik_f[0:1]))
            seq(v.tensor_scalar(ring_i, ring_i, 4 * CH - 1, None, ALU.bitwise_and))
            seq(v.memset(pair_tab[:, :, :, :], 0))
            seq(v.tensor_copy(pair_tab[:, :, 0:2, 0:STEPS].rearrange("p a b c -> p (a b) c") if False else
                              pair_tab[:, :, 0:2, 0:STEPS], ring_i.rearrange("p (a b c) -> p a b c", b=2, c=STEPS)))
            j4 = jk_f[0:1].rearrange("p (a b c) -> p a b c", b=2, c=STEPS)
            seq(v.tensor_copy(tile_tab[:, :, 0:2], j4[:, :, :, 0]))
            seq(v.tensor_tensor(ik_f[0:1].rearrange("p (a b c) -> p a b c", b=2, c=STEPS), j4,
                                j4[:, :, :, 0:1].to_broadcast([1, ROUNDS, 2, STEPS]), ALU.subtract))
            seq(v.tensor_copy(pair_tab[:, :, 2:4, 0:STEPS],
                              ik_f[0:1].rearrange("p (a b c) -> p a b c", b=2, c=STEPS)))
            seq(v.tensor_scalar(chunk_i[:, 0], chunk_i[:, 0], 7, None, ALU.logical_shift_right))
            seq(v.tensor_copy(chunk_f, chunk_i[:, 0]))
            seq(v.tensor_scalar(chunk_f, chunk_f, float(NTR - 1), None, ALU.min))
            seq(v.tensor_tensor(chunk_f, chunk_f, chunk_k, ALU.add))
            seq(v.tensor_copy(round_c, round_i))
            seq(v.tensor_tensor(round_c, round_c, chunk_f[:, :, None].to_broadcast([1, NCH, ROUNDS]), ALU.is_le))
            seq(v.tensor_reduce(round_f, round_c, AX, ALU.add))
            seq(v.memset(round_tab[:, :], 0))
            seq(v.tensor_copy(round_tab[:, 1:NCH + 1], round_f))
            seq(v.memset(round_tab[:, NCH:NCH + 1], ROUNDS))
            seq(v.tensor_tensor(goes_on[:, :], chunk_i[:, 1], chunk_i[:, 2], ALU.is_equal))
            seq(v.tensor_tensor(win_f, win_i[:, :, 1:P + 2], win_i[:, :, 0:P + 1], ALU.is_equal))
            seq(v.tensor_scalar(same_prev[:, :, :], win_f[:, :, 0:P], 1.0, BIG, ALU.subtract, ALU.mult))
            seq(v.tensor_scalar(same_next[:, :, :], win_f[:, :, 1:P + 1][:, :, ::-1], 1.0, BIG,
                                ALU.subtract, ALU.mult))
            seq(v.tensor_tensor(row_f[:, :], ends_i[:, 0, 1:], ends_i[:, 0, :ET], ALU.is_equal))
            seq(v.tensor_scalar(row_f[:, :], row_f[:, :], 1.0, BIG, ALU.subtract, ALU.mult))
            seq(v.tensor_tensor(ends_f, ends_i[:, 1, 1:], ends_i[:, 1, :ET], ALU.is_equal))
            seq(v.tensor_scalar(row_b[:, :].rearrange("p (c t) -> p c t", t=CH),
                                ends_f.rearrange("p (c t) -> p c t", t=CH)[:, :, ::-1], 1.0, BIG,
                                ALU.subtract, ALU.mult))
            seq(v.tensor_tensor(last_edge[:, :], cols_i[:, 0], cols_i[:, 1], ALU.not_equal))
            seq(v.tensor_tensor(ccol[:, 0], cols_i[:, 0], cols_i[:, 2], ALU.is_equal))
            seq(v.tensor_tensor(ccol[:, 1], cols_i[:, 2], cols_i[:, 3], ALU.is_equal))
            seq(v.tensor_tensor(crosses[:, :], ccol[:, 0], ccol[:, 1], ALU.mult))
            dve.wait_ge(prep_t, 4)
            seq(v.tensor_tensor(pw[:, :, 2 * C:], pw[:, :, 0:C], pw[:, :, C:2 * C], ALU.add))
            seq(v.tensor_tensor(pw[:, :, 2 * C:], pw[:, :, 2 * C:],
                                bank[6][0:C + 1, 0:GAT * C].rearrange("p (a b) -> p a b", a=GAT), ALU.add))
            seq(v.memset(h_t[C:C + 1, :, :], 1.0))
            seq(v.memset(bwd_row[:, :], -BIG))
            seq(v.memset(eps_c[:, :], EPS))
            seq(v.memset(w0[:, C:], 0.0))
            for s in (*hot_done, *win_done, *add_done):
                v.memset(less_max[:, 0:1], 0.0).then_inc(s, 1)
                dve.wait_ge(s, 1)
            seq(v.memset(spare, 0.0))
            seq(v.memset(scratch, 0.0))
            assert step[0] == PV["all"], step

            def rounds(layer, c):
                lo = dve.value_load(round_tab[0:1, ds(c, 1)], min_val=0, max_val=ROUNDS)
                hi = dve.value_load(round_tab[0:1, ds(c + 1, 1)], min_val=0, max_val=ROUNDS)
                with dve.Fori(lo, hi) as r:
                    g = r + (ROUNDS * layer + 1)
                    _, first = nc.values_load_multi_w_load_instructions(
                        tile_tab[0:1, ds(r, 1), 0:2].rearrange("p a b -> p (a b)"),
                        engines=(DVE,), min_val=0, max_val=NTR - 1,
                        skip_runtime_bounds_check_because=CLAMPED)
                    for b in range(2):
                        dve.wait_ge(win_done[b], g + 1)
                        dve.wait_ge(add_done[1 - b], g + b)
                        table = nodes[:, ds(first[b], STEPS), :]
                        v.tensor_tensor(table, table,
                                        win_ps[b][:, 0:STEPS * W].rearrange("p (t w) -> p t w", t=STEPS),
                                        ALU.add).then_inc(add_done[b], 1)
                        dve.wait_ge(hot_done[b], g + 1)
                        one_hot(b, r * PAIRS + (PAIRS + b * STEPS))

            def one_hot(b, first_pair):
                v.tensor_tensor(hot[b][:, :, :], iota_f[:, None, :].to_broadcast([P, STEPS, P]),
                                dst_rel[:, ds(first_pair, STEPS)][:, :, None].to_broadcast([P, STEPS, P]),
                                ALU.is_equal).then_inc(hot_done[b], 1)

            def edge_phase(layer):
                def scores(it, k):
                    kk = k + NCH * layer
                    n1 = 4 * it + kk - NCH
                    c = 4 * it + k
                    for q in range(QCH):
                        nq = 4 * n1 + q
                        dve.wait_ge(relu_done, nq + 1)
                        w(dve, att_done, nq - 1)
                        v.scalar_tensor_tensor(out=leaky[:, q % 2], in0=z_ps[q % 2][:, 0:QUAD * C].rearrange("p (t c) -> p t c", t=QUAD),
                                               scalar=SLOPE, in1=relu_z[:, q % 2], op0=ALU.mult,
                                               op1=ALU.add).then_inc(leaky_done, 1)
                        dve.wait_ge(leaky_done, nq + 1)
                        w(dve, score_done, nq - 1)
                        v.tensor_tensor(weighted[:, q % 2], leaky[:, q % 2],
                                        att_b[:, layer - 1:layer, :].to_broadcast([P, QUAD, C]),
                                        ALU.mult).then_inc(att_done, 1)
                        dve.wait_ge(att_done, nq + 1)
                        w(dve, less_done, n1 - 1)
                        v.tensor_reduce(score[:, kk % 2, q * QUAD:(q + 1) * QUAD], weighted[:, q % 2],
                                        AX, ALU.add).then_inc(score_done, 1)
                    dve.wait_ge(score_t, n1 + 1)
                    w(dve, scans2, 2 * n1)
                    w(dve, max_done, n1)
                    flags_f = same_prev[:, ds(c, 1), :].rearrange("p a b -> p (a b)")
                    flags_b = same_next[:, ds(c, 1), :].rearrange("p a b -> p (a b)")
                    st = tr_ps[0:CH, 0:P]
                    v.tensor_tensor_scan(scan_f[:, :], flags_f, st, -BIG, ALU.add, ALU.max).then_inc(scans, 1)
                    v.tensor_tensor_scan(scan_b[:, :][:, ::-1], flags_b, st[:, ::-1], -BIG, ALU.add,
                                         ALU.max).then_inc(scans, 1)
                    here, other = fwd_row[:, kk % 2], fwd_row[:, 1 - kk % 2]
                    w(dve, arg_done, n1)
                    w(dve, rows_done, 3 * n1)
                    if isinstance(it, int) and k == 0:
                        v.memset(here[:, 0:1], -BIG).then_inc(rows_done, 1)
                    else:
                        v.tensor_copy(here[:, 0:1], other[:, CH:CH + 1]).then_inc(rows_done, 1)
                    dve.wait_ge(ends_t, n1 + 1)
                    v.tensor_tensor_scan(bwd_row[:, 0:CH][:, ::-1], row_b[:, ds(c * CH, CH)],
                                         row_ps[0:1, CH:2 * CH][:, ::-1], -BIG, ALU.add,
                                         ALU.max).then_inc(rows_done, 1)
                    dve.wait_ge(rows_done, 3 * n1 + 1)
                    v.tensor_tensor_scan(here[:, 1:CH + 1], row_f[:, ds(c * CH, CH)],
                                         row_ps[0:1, 0:CH], here[:, 0:1], ALU.add, ALU.max).then_inc(rows_done, 1)
                    dve.wait_ge(rows_t, n1 + 1)
                    dve.wait_ge(scans, 2 * (n1 + 1))
                    v.tensor_copy(init[:, :], row_ps[0:CH, 32:34]).then_inc(init_done, 1)
                    dve.wait_ge(init_done, n1 + 1)
                    v.tensor_tensor_scan(scan_f[:, :], flags_f, st, init[:, 0:1], ALU.add, ALU.max).then_inc(scans2, 1)
                    v.tensor_tensor_scan(scan_b[:, :][:, ::-1], flags_b, st[:, ::-1], init[:, 1:2], ALU.add,
                                         ALU.max).then_inc(scans2, 1)
                    dve.wait_ge(scans2, 2 * (n1 + 1))
                    w(dve, max_t, n1)
                    v.tensor_tensor(seg_max[:, :], scan_f[:, :], scan_b[:, :], ALU.max).then_inc(max_done, 1)
                    dve.wait_ge(max_done, n1 + 1)
                    w(dve, rescale_done, n1)
                    v.scalar_tensor_tensor(out=neg_arg[:, :], in0=seg_max[0:1, 0:1], scalar=here[:, 0:1],
                                           in1=goes_on[:, ds(c, 1)], op0=ALU.subtract,
                                           op1=ALU.mult).then_inc(arg_done, 1)
                    dve.wait_ge(max_t, n1 + 1)
                    w(dve, exp_done, n1)
                    top = row_ps[:, 64:64 + CH]
                    v.tensor_tensor(less_max[:, :], score[:, kk % 2, :], top, ALU.subtract).then_inc(less_done, 1)
                    w(dve, carry_done, 4 * it + kk - 1)
                    ring = (k % 4) * CH
                    flag = last_edge[:, ds(c * CH, CH)]
                    v.tensor_copy(msg[:, ring:ring + CH, LAST], flag).then_inc(flags_done, 1)
                    v.tensor_tensor(msg[:, ring:ring + CH, MAXI], flag, top, ALU.mult).then_inc(flags_done, 1)

                def body(it, k):
                    kk = k + NCH * layer
                    n = 4 * it + kk
                    c = 4 * it + k
                    first = isinstance(it, int) and k == 0
                    if layer:
                        scores(it, k)
                    w(dve, carry_done, n - 1)
                    v.tensor_copy(cross_ring[:, kk % 2, :], crosses[:, ds(c * CH, CH)]).then_inc(cross_done, 1)
                    if not first:
                        rounds(layer, c - 1)
                        dve.wait_ge(msg_done, n + 1)
                        dve.wait_ge(carry_done, n)
                        if layer:
                            dve.wait_ge(rescale_done, n - NCH + 1)
                        ring = (k % 4) * CH
                        v.scalar_tensor_tensor(out=msg[0:1, ring, 0:C + 1], in0=carry_ps[0:1, 0:C + 1],
                                               scalar=rescale[:, 0:1] if layer else 1.0,
                                               in1=msg[0:1, ring, 0:C + 1], op0=ALU.mult,
                                               op1=ALU.add).then_inc(carried, 1)

                if layer:
                    dve.wait_ge(cleared, UNITS * layer)
                chunk_loop(dve, body, layer)
                rounds(layer, NCH - 1)

            def node_phase(layer):
                n0 = UNITS * layer
                nn = UNITS * (layer - 1)
                ln0 = 0 if layer == 0 else UNITS

                def coefficients():
                    base = [10 * (layer - 1)]

                    def cs(ins):
                        base[0] += 1
                        ins.then_inc(coef_v, 1)
                        dve.wait_ge(coef_v, base[0])
                    t1 = region[:, 0:NT]
                    t2 = region[:, NT:2 * NT]
                    dve.wait_ge(add_done[0], ROUNDS * (layer + 1) + 1)
                    dve.wait_ge(add_done[1], ROUNDS * (layer + 1) + 1)
                    cs(v.tensor_scalar(t1, nodes[:, :, LAST], BIG, BIG, ALU.mult, ALU.subtract))
                    cs(v.tensor_tensor(t1, t1, nodes[:, :, MAXI], ALU.add))
                    cs(v.tensor_tensor(t2, t1, self_score[:, :], ALU.max))
                    v.tensor_tensor(c_edge[:, :], t1, t2, ALU.subtract)
                    cs(v.tensor_tensor(c_self[:, :], self_score[:, :], t2, ALU.subtract))
                    dve.wait_ge(coef_a, 2 * layer)
                    cs(v.tensor_tensor(t1, c_edge[:, :], nodes[:, :, WGT], ALU.mult))
                    cs(v.tensor_tensor(t1, t1, c_self[:, :], ALU.add))
                    cs(v.tensor_scalar(t1, t1, 1e-16, None, ALU.add))
                    cs(v.reciprocal(t2, t1))
                    cs(v.tensor_tensor(c_edge[:, :], c_edge[:, :], t2, ALU.mult))
                    cs(v.tensor_tensor(c_self[:, :], c_self[:, :], t2, ALU.mult))

                def edge_share(u, s, n):
                    if layer < GAT:
                        w(dve, h_t_done, n0 + u - 3)
                    q = ds(QUAD * u, QUAD)
                    v.tensor_tensor(h[:, s], nodes[:, q, 0:C],
                                    c_edge[:, q][:, :, None].to_broadcast([P, QUAD, C]),
                                    ALU.mult).then_inc(edge_part, 1)

                def new_rows(u, s, n):
                    dve.wait_ge(edge_part, nn + u + 1)
                    dve.wait_ge(self_part, nn + u + 1)
                    v.tensor_tensor(h[:, s], h[:, s], t_self[:, s], ALU.add).then_inc(h_done, 1)

                def rows_of(s):
                    if layer == 0:
                        return y_ps[s % 2][:, 0:QUAD * Y].rearrange("p (t c) -> p t c", t=QUAD)[:, :, 0:C]
                    return h[:, s]

                def total(u, s, n):
                    if layer == 0:
                        dve.wait_ge(y_done, u + 1)
                    else:
                        dve.wait_ge(h_done, nn + u + 1)
                    v.tensor_reduce(stat[:, s, 0], rows_of(s), AX, ALU.add).then_inc(mean_sum, 1)

                def center(u, s, n):
                    dve.wait_ge(mean_sum, ln0 + u + 1)
                    w(dve, norm_done, ln0 + u - 3)
                    v.scalar_tensor_tensor(out=centered[layer // GAT][:, s],
                                           in0=stat[:, s, 0][:, :, None].to_broadcast([P, QUAD, C]),
                                           scalar=-1.0 / C, in1=rows_of(s), op0=ALU.mult,
                                           op1=ALU.add).then_inc(center_done, 1)

                def variance(u, s, n):
                    dve.wait_ge(square_done, ln0 + u + 1)
                    v.tensor_reduce(stat[:, s, 1], leaky[:, s % 2], AX, ALU.add).then_inc(var_done, 1)

                def inverse(u, s, n):
                    dve.wait_ge(dev_done, ln0 + u + 1)
                    v.reciprocal(stat[:, s, 3], stat[:, s, 2]).then_inc(inv_done, 1)

                def scale(u, s, n):
                    dve.wait_ge(inv_done, ln0 + u + 1)
                    if layer == 0:
                        w(dve, h_t_done, u - 3)
                    w(dve, norm_out[s], (PER_LAYER // 2 if layer else 0) + 16 * (n - 1))
                    v.tensor_tensor(normed[layer // GAT][:, s], centered[layer // GAT][:, s],
                                    stat[:, s, 3][:, :, None].to_broadcast([P, QUAD, C]),
                                    ALU.mult).then_inc(norm_done, 1)

                def self_leaky(u, s, n):
                    dve.wait_ge(proj_copied, 2 * (n0 + u + 1))
                    w(dve, s_att, n0 + u - 1)
                    z = projected[:, s, :, 2 * C:]
                    v.scalar_tensor_tensor(out=relu_z[:, s % 2], in0=z, scalar=SLOPE, in1=z, op0=ALU.mult,
                                           op1=ALU.max).then_inc(s_leaky, 1)

                def self_att(u, s, n):
                    dve.wait_ge(s_leaky, n0 + u + 1)
                    w(dve, s_score, n0 + u - 1)
                    v.tensor_tensor(weighted[:, s % 2], relu_z[:, s % 2],
                                    att_b[:, layer:layer + 1, :].to_broadcast([P, QUAD, C]),
                                    ALU.mult).then_inc(s_att, 1)

                def self_sum(u, s, n):
                    dve.wait_ge(s_att, n0 + u + 1)
                    v.tensor_reduce(self_score[:, ds(QUAD * u, QUAD)], weighted[:, s % 2], AX,
                                    ALU.add).then_inc(s_score, 1)

                if layer == 0:
                    unit_loop(dve, [(8, inverse), (4, total), (13, self_leaky), (8, scale), (13, self_att),
                                    (4, center), (6, variance), (13, self_sum)])
                elif layer < GAT:
                    coefficients()
                    unit_loop(dve, [(8, self_leaky), (2, edge_share), (8, self_att), (3, new_rows),
                                    (8, self_sum)])
                else:
                    coefficients()
                    unit_loop(dve, [(8, inverse), (4, total), (2, edge_share), (8, scale), (3, new_rows),
                                    (4, center), (6, variance)])

            for b in range(2):
                one_hot(b, b * STEPS)
            for layer in range(LAYERS):
                edge_phase(layer)
                node_phase(layer)


PER_LAYER = 32 * (UNITS // 4)
PE = mybir.EngineType.PE
DVE = mybir.EngineType.DVE
PV = {"before": 12, "pick": 23, "fold": 31, "we": 33, "all": 73}


def kernel(**inputs):
    import concourse.bacc as bacc
    from concourse.bass_utils import run_bass_kernel_spmd

    a = {k: np.ascontiguousarray(v) for k, v in inputs.items()}
    pad = ROWS - E

    def padded(v, fill):
        return np.pad(v, [(0, pad)] + [(0, 0)] * (v.ndim - 1), constant_values=fill)

    def columns(v):
        return np.ascontiguousarray(v.reshape(ET, P).T)

    dst, src = padded(a["dst"], FAR), padded(a["src"], 0)
    dst_g = padded(a["dst"], 0)
    after = np.concatenate([dst[1:], [-1]]).astype(np.int32)
    around = np.concatenate([[-1], dst, [-1]]).astype(np.int32)
    chunk = CH * P
    c_last = np.repeat(dst[chunk - 1::chunk], chunk)
    c_next = np.repeat(after[chunk - 1::chunk], chunk)
    start = P * (np.arange(CH)[:, None] + CH * np.arange(NCH)[None, :])
    ins = {
        "x": padded(a["x"], 0),
        "edge_idx": np.ascontiguousarray(
            np.stack([src, dst_g]).reshape(2, NCH, CH, P).transpose(1, 3, 0, 2)),
        "tile_last": np.ascontiguousarray(dst[P - 1::P].reshape(SELQ, SELP).T),
        "row_dst": dst.reshape(ET, P), "row_clast": c_last.reshape(ET, P), "row_cnext": c_next.reshape(ET, P),
        "col_ids": np.stack([columns(v) for v in (dst, after, c_last, c_next)]),
        "win_dst": around[start[:, :, None] + np.arange(P + 2)],
        "row_ends": np.stack([around[0::P][:ET + 1], around[1::P][:ET + 1]])[None],
        "chunk_ends": np.stack([dst[chunk - 1::chunk], around[0::chunk][:NCH], around[1::chunk][:NCH]])[None],
        "col_weight": columns(padded(a["edge_weight"], 0)),
        "attr_t": np.concatenate([padded(a["edge_attr_32"], 0).T, np.ones((1, ROWS), np.float32)]),
        "emb_t": np.ascontiguousarray(np.concatenate([a["L1_gnn_W_emb"], a["L1_gnn_b_emb"][None]]).T),
        "We": a["L1_gnn_We"], "Wl": a["L1_gnn_Wl"], "Wr": a["L1_gnn_Wr"], "bl": a["L1_gnn_bl"],
        "br": a["L1_gnn_br"], "W0": a["L0_gnn_W"], "b0": a["L0_gnn_b"], "att": a["L1_gnn_att"],
        "bias": a["L1_gnn_bias"], "bias_t": np.ascontiguousarray(a["L1_gnn_bias"].T),
    }
    nc = bacc.Bacc("TRN2", target_bir_lowering=False, num_devices=1)
    io = {k: nc.dram_tensor(f"in_{k}", v.shape, mybir.dt.from_np(v.dtype), kind="ExternalInput").ap()
          for k, v in ins.items()}
    io["out"] = nc.dram_tensor("out_x", (ROWS, C), F32, kind="ExternalOutput").ap()
    build(nc, io)
    r = run_bass_kernel_spmd(nc, [{f"in_{k}": v for k, v in ins.items()}], core_ids=[0])
    return r.results[0]["out_x"][:N]
```

```python
from contextlib import ExitStack

import numpy as np
import concourse.bass as bass
from concourse import mybir

F32 = mybir.dt.float32
BF16 = mybir.dt.bfloat16
I32 = mybir.dt.int32
I16 = mybir.dt.int16
ALU = mybir.AluOpType
ACT = mybir.ActivationFunctionType
AX = mybir.AxisListType.X
ds = bass.ds

P = 128
N = 50000
E = 50000
C = 64
R = 32
GAT = 3
LAYERS = 1 + GAT
CH = 16
NCH = -(-E // (P * CH))
ET = NCH * CH
NT = ET
ROWS = ET * P
NTR = -(-N // P)
STEPS = 5
PAIRS = 2 * STEPS
ROUNDS = -(-(ET + NTR - 1) // PAIRS)
K = ROUNDS * PAIRS
W = 96
NW = 68
WGT, LAST, MAXI = C, C + 1, C + 2
SELP = 100
SELQ = ET // SELP
QUAD = 4
QCH = CH // QUAD
UNITS = NT // QUAD
BIG = 1e30
FAR = 1 << 17
SLOPE = 0.2
EPS = 1e-5
Y = 96
CLAMPED = "the preparation clamps the tables' values to the shapes' bounds"
PROJ = 3 * C


def w(eng, sem, value):
    if not isinstance(value, int) or value > 0:
        eng.wait_ge(sem, value)


def waits_apart(eng, reached, *waits):
    known = [(sem, v if isinstance(v, int) else eng.to_reg(v)) for sem, v in waits]
    eng.wait_ge(reached, 1)
    for sem, v in known:
        if not isinstance(v, int) or v > 0:
            eng.wait_ge(sem, v)


def chunk_loop(eng, body, layer):
    peeled = 1 if layer == 0 else 0
    body(0, 0)
    for it in range(peeled):
        for k in range(1, 5):
            body(it, k)
    with eng.Fori(peeled, (NCH - 1) // 4) as it:
        for k in range(1, 5):
            body(it, k)


def unit_loop(eng, stages):
    def turn(four, r):
        for lag, stage in stages:
            if isinstance(four, int) and not 0 <= 4 * four + r - lag < UNITS:
                continue
            stage(4 * four + (r - lag), (r - lag) % 4, four + (r - lag) // 4 + 1)
    lags = max(lag for lag, _ in stages)
    peeled = -(-lags // 4) + 1
    for x in range(peeled):
        for r in range(4):
            turn(x, r)
    with eng.Fori(peeled, UNITS // 4) as it:
        for r in range(4):
            turn(it, r)
    for r in range(lags):
        turn(UNITS // 4 + r // 4, r % 4)


def build(nc, io):
    ctx = ExitStack()
    with ctx:
        def sb(name, shape, dt=F32):
            return ctx.enter_context(nc.sbuf_tensor(name, shape, dt))

        def sem(name):
            return ctx.enter_context(nc.semaphore(name))

        def dram(name, shape, dt=F32):
            return nc.dram_tensor(name, shape, dt, kind="Internal").ap()

        xl_tab = [dram(f"xl_tab{i}", (ROWS, C)) for i in range(2)]
        xr_tab = [dram(f"xr_tab{i}", (ROWS, C)) for i in range(2)]
        x1_tab = dram("x1_tab", (ROWS, C))

        def unit_rows(tab, u):
            return tab.rearrange("(t p) c -> p t c", p=P)[:, ds(QUAD * u, QUAD), :]

        nodes = sb("nodes", [P, NT, NW])
        msg = sb("msg", [P, 4 * CH, W])
        dst_rel = sb("dst_rel", [P, K + PAIRS])
        same_prev = sb("same_prev", [CH, NCH, P], BF16)
        same_next = sb("same_next", [CH, NCH, P], BF16)
        edge_idx = sb("edge_idx", [P, 4, 2, CH], I32)
        last_edge = sb("last_edge", [P, ET], BF16)
        crosses = sb("crosses", [P, ET], BF16)
        cross_ring = sb("cross_ring", [P, 2, CH])
        row_f = sb("row_f", [1, ET])
        row_b = sb("row_b", [1, ET])
        goes_on = sb("goes_on", [1, NCH])
        pair_tab = sb("pair_tab", [1, ROUNDS, 4, STEPS], I16)
        tile_tab = sb("tile_tab", [1, ROUNDS, 4], I32)
        round_tab = sb("round_tab", [1, 32], I32)
        hot = [sb(f"hot{i}", [P, STEPS, P]) for i in range(2)]
        ident = sb("ident", [P, P])
        iota_f = sb("iota_f", [P, P])
        part_id = sb("part_id", [P, 1])
        zero_row = sb("zero_row", [P, NW])
        zeros_b = sb("zeros_b", [1, 512], BF16)
        we = sb("we", [R + 1, GAT, Y])
        pw = sb("pw", [C + 1, GAT, PROJ])
        w0 = sb("w0", [2 * C, 2 * C])
        att_b = sb("att_b", [P, GAT, C])
        bias_c = sb("bias_c", [C, GAT])
        bias_b = sb("bias_b", [P, C])
        bias0_b = sb("bias0_b", [P, C])
        self_score = sb("self_score", [P, NT])
        c_edge = sb("c_edge", [P, NT])
        weight = c_edge
        c_self = sb("c_self", [P, NT])
        score = sb("score", [P, 2, CH])
        scan_f = sb("scan_f", [CH, P])
        scan_b = sb("scan_b", [CH, P])
        seg_max = sb("seg_max", [CH, P])
        fwd_row = sb("fwd_row", [1, 2, CH + 1])
        bwd_row = sb("bwd_row", [1, CH + 1])
        neg_arg = sb("neg_arg", [1, 1])
        rescale = sb("rescale", [1, 1])
        less_max = sb("less_max", [P, CH])
        init = sb("init", [CH, 2])
        eps_c = sb("eps_c", [P, 1])
        stat = sb("stat", [P, 4, 4, QUAD])

        region = sb("region", [P, 8192])

        def part(at, n, shape, rows=P):
            v = region[0:rows, at:at + n]
            names = " ".join("abcd"[:len(shape)])
            return v.rearrange(f"p ({names}) -> p {names}", **dict(zip("abcd", shape)))

        gathered = part(0, 2048, (2, CH, C))
        gathered_r = part(2048, 2048, (2, CH, C))
        leaky_e = part(6144, 1024, (QCH, QUAD, C))
        weighted_e = part(7168, 1024, (QCH, QUAD, C))
        attr = part(4096, 2048, (4, 512), R + 1)
        h = part(0, 1024, (4, QUAD, C))
        t_self = part(1024, 1024, (4, QUAD, C))
        loaded = part(2048, 1024, (4, QUAD, C))
        projected = part(3072, 3072, (4, QUAD, PROJ))
        f_cols = part(6144, 512, (2, 2, P))
        h_t = part(7168, 1024, (2, 512), C + 1)
        idle = msg[:, CH:, :].rearrange("p t w -> p (t w)")[:, 0:8 * QUAD * C].rearrange(
            "p (x s t c) -> p x s t c", x=4, s=2, t=QUAD)
        sums, squares, leaky_s, weighted_s = (idle[:, x] for x in range(4))
        centered = [t_self, part(6144, 1024, (4, QUAD, C))]
        normed = [h, part(7168, 1024, (4, QUAD, C))]

        bank = [ctx.enter_context(nc.psum_tensor(f"bank{i}", [P, 512], F32)) for i in range(8)]
        z_ps = bank[0:2]
        tr_ps = bank[2]
        row_ps = bank[3]
        win_ps = bank[4:6]
        carry_ps = bank[6]
        ht_ps = bank[0:2]
        y_ps = bank[2:4]
        pj_ps = bank[4:8]

        loads = sem("loads")
        attr_loads = sem("attr_loads")
        consts = sem("consts")
        prep_v = sem("prep_v")
        zeroed = sem("zeroed")
        prep_t = sem("prep_t")

        scratch = nodes[:, :, :].rearrange("p t w -> p (t w)")
        spare = msg[:, :, :].rearrange("p t w -> p (t w)")
        at = [0]

        def temp(shape, dt=F32, rows=P, place=None):
            n = int(np.prod(shape))
            words = n if dt in (F32, I32) else -(-n // 2)
            if place is None:
                v = scratch[0:rows, at[0]:at[0] + words]
                at[0] += words
            else:
                v = place[0:rows, 0:words]
            if dt is not F32:
                v = v.bitcast(dt)
            if len(shape) > 1:
                names = " ".join("abcd"[:len(shape)])
                v = v.rearrange(f"p ({names}) -> p {names}", **dict(zip("abcd", shape)))
            return v

        HALF = E // 8
        last_i = temp((SELQ,), I32, SELP)
        rows_i = temp((3, SELQ, P), I32, SELP, region[:, HALF:HALF + 3 * SELQ * P])
        drow = temp((SELQ, P), F32, SELP)
        drow2 = temp((SELQ, P), F32, SELP)
        v_f = temp((SELQ,), F32, SELP)
        before = temp((SELQ, K), BF16, SELP)
        pick = temp((SELQ, K), F32, SELP)
        ones_b = temp((P,), BF16, SELP)
        attr_a = temp((HALF,), F32, P, region)
        attr_b = temp((HALF,))
        early_end = at[0]
        cols_i = temp((4, ET), I32)
        ccol = temp((2, ET))
        win_i = temp((NCH, P + 2), I32, CH)
        win_f = temp((NCH, P + 1), F32, CH)
        ends_i = temp((2, ET + 1), I32, 1)
        ends_f = temp((ET,), F32, 1)
        chunk_i = temp((3, NCH), I32, 1)
        chunk_f = temp((NCH,), F32, 1)
        round_i = temp((NCH, ROUNDS), I32, 1, spare)
        round_c = temp((NCH, ROUNDS), F32, 1, spare[:, NCH * ROUNDS:])
        round_f = temp((NCH,), F32, 1)
        tile_i = temp((SELQ,), I32)
        tile_f = temp((SELQ,))
        k_i = temp((K,), I32)
        k_f = temp((K,))
        ik_f = temp((K,))
        jk_f = temp((K,))
        ring_i = temp((K,), I32, 1)
        chunk_k = temp((NCH,), I32, 1)
        iota_i = temp((P,), I32)
        pid_i = temp((1,), I32)
        attr_sum = temp((1,))
        attr_sum2 = temp((1,))
        fold = temp((R,))
        mean_c = temp((C + 1,), F32, R + 1)
        emb_t = temp((R + 1,), F32, C)
        we_in = temp((GAT, C), F32, C)
        late_end = at[0]
        late_mid = early_end + (late_end - early_end) * 3 // 4
        assert late_end <= NT * NW
        HK = K // 2

        N_LOADS = 21

        idx_in = [sem(f"idx_in{i}") for i in range(4)]
        gat_in = [sem(f"gat_in{i}") for i in range(8)]
        attr_in = [sem(f"attr_in{i}") for i in range(4)]
        z_done = sem("z_done")
        sum_done = sem("sum_done")
        z_read = sem("z_read")
        leaky_done = sem("leaky_done")
        att_done = sem("att_done")
        score_done = sem("score_done")
        score_t = sem("score_t")
        scans = sem("scans")
        ends_t = sem("ends_t")
        rows_done = sem("rows_done")
        rows_t = sem("rows_t")
        init_done = sem("init_done")
        scans2 = sem("scans2")
        max_done = sem("max_done")
        arg_done = sem("arg_done")
        max_t = sem("max_t")
        less_done = sem("less_done")
        flags_done = sem("flags_done")
        rescale_done = sem("rescale_done")
        exp_done = sem("exp_done")
        msg_done = sem("msg_done")
        cross_done = sem("cross_done")
        carried = sem("carried")
        carry_done = sem("carry_done")
        hot_done = [sem(f"hot_done{i}") for i in range(2)]
        win_done = [sem(f"win_done{i}") for i in range(2)]
        add_done = [sem(f"add_done{i}") for i in range(2)]

        row_in = [sem(f"row_in{i}") for i in range(4)]
        res_in = [sem(f"res_in{i}") for i in range(4)]
        row_out = [sem(f"row_out{i}") for i in range(4)]
        norm_out = [sem(f"norm_out{i}") for i in range(4)]
        copy_done = sem("copy_done")
        row_biased = sem("row_biased")
        f_t = sem("f_t")
        f_t_copied = sem("f_t_copied")
        y_done = sem("y_done")
        mean_sum = sem("mean_sum")
        center_done = sem("center_done")
        square_done = sem("square_done")
        var_done = sem("var_done")
        dev_done = sem("dev_done")
        inv_done = sem("inv_done")
        norm_done = sem("norm_done")
        coef_v = sem("coef_v")
        coef_a = sem("coef_a")
        edge_part = sem("edge_part")
        self_part = sem("self_part")
        cleared = sem("cleared")
        ones_set = sem("ones_set")
        h_done = sem("h_done")
        h_t_done = sem("h_t_done")
        h_t_copied = sem("h_t_copied")
        proj_done = sem("proj_done")
        proj_copied = sem("proj_copied")
        s_leaky = sem("s_leaky")
        s_att = sem("s_att")
        s_score = sem("s_score")
        res_added = sem("res_added")

        EVEN = [(NCH + 1) // 2, NCH // 2]

        def gath_target(layer, it, k, q):
            kk = k + NCH * layer
            uses = 2 * it + kk // 2 + 1
            if layer == 0:
                return uses * 16 * QUAD
            return 16 * QUAD * EVEN[kk % 2] + (uses - EVEN[kk % 2]) * 32 * QUAD

        block = ctx.enter_context(nc.Block())

        @block.sync
        def _(sp):
            def load(to, frm):
                sp.dma_start(to, frm).then_inc(loads, 16)

            load(last_i, io["tile_last"])
            load(rows_i[:, 0], io["row_dst"].rearrange("(q p) l -> p q l", p=SELP))
            load(rows_i[:, 1], io["row_clast"].rearrange("(q p) l -> p q l", p=SELP))
            load(rows_i[:, 2], io["row_cnext"].rearrange("(q p) l -> p q l", p=SELP))
            load(cols_i, io["col_ids"].rearrange("a p t -> p a t"))
            load(win_i, io["win_dst"])
            load(ends_i, io["row_ends"])
            load(chunk_i, io["chunk_ends"])
            load(weight[:, :], io["col_weight"])
            load(emb_t, io["emb_t"])
            load(we_in, io["We"].rearrange("l k c -> k l c"))
            load(pw[0:C, :, 0:C], io["Wl"].rearrange("l k c -> k l c"))
            load(pw[0:C, :, C:2 * C], io["Wr"].rearrange("l k c -> k l c"))
            load(pw[C:C + 1, :, 0:C], io["bl"][None])
            load(pw[C:C + 1, :, C:2 * C], io["br"][None])
            load(w0[0:C, 0:C], io["W0"])
            load(w0[C:2 * C, C:2 * C], io["W0"])
            load(bias0_b[:, :], io["b0"][None].to_broadcast([P, C]))
            load(att_b[:, :, :], io["att"][None].to_broadcast([P, GAT, C]))
            load(bias_c[:, :], io["bias_t"])
            load(bias_b[:, :], io["bias"][GAT - 1:GAT, :].to_broadcast([P, C]))
            for s in range(4):
                for half, to in enumerate((attr_a, attr_b)):
                    at = (2 * s + half) * HALF
                    sp.dma_start(to[s * R:(s + 1) * R], io["attr_t"][0:R, at:at + HALF]).then_inc(attr_loads, 16)

            def edge_phase(layer):
                def idx(it, k):
                    kk = k + NCH * layer
                    w(sp, msg_done, 4 * it + kk - 3)
                    sp.dma_start(edge_idx[:, kk % 4], io["edge_idx"][ds(4 * it + k, 1)].rearrange(
                        "o p a t -> (o p) a t")).then_inc(idx_in[kk % 4], 16)

                def body(it, k):
                    idx(it, k)
                    if layer == 0:
                        return
                    for q in range(QCH):
                        n = 4 * (4 * it + k + NCH * (layer - 1)) + q
                        w(sp, z_done, n - 3)
                        sp.dma_start(attr[:, q, :], io["attr_t"][:, ds((4 * it + k) * CH * P + q * 512, 512)]
                                     ).then_inc(attr_in[q], 16)
                if layer:
                    for s in range(4):
                        sp.wait_ge(row_out[s], PER_LAYER * layer)
                        sp.wait_ge(norm_out[s], PER_LAYER // 2)
                    sp.wait_ge(s_score, UNITS * layer)
                chunk_loop(sp, body, layer)

            def node_phase(layer):
                n0 = UNITS * layer
                cur = (layer - 1) % 2
                nxt = layer % 2

                def fetch(u, s, n):
                    if layer == 0:
                        w(sp, y_done, u - 3)
                        sp.dma_start(loaded[:, s], unit_rows(io["x"], u)).then_inc(row_in[s], 16)
                    else:
                        w(sp, self_part, UNITS * (layer - 1) + u - 3)
                        sp.dma_start(loaded[:, s], unit_rows(xl_tab[cur], u)).then_inc(row_in[s], 16)
                    if layer == GAT:
                        sp.dma_start(projected[:, s, :, 0:C], unit_rows(x1_tab, u)).then_inc(res_in[s], 16)

                def store_norm(u, s, n):
                    sp.wait_ge(norm_done, (0 if layer == 0 else UNITS) + u + 1)
                    to = x1_tab if layer == 0 else io["out"]
                    sp.dma_start(unit_rows(to, u), normed[layer // GAT][:, s]).then_inc(norm_out[s], 16)

                def store_proj(u, s, n):
                    sp.wait_ge(proj_copied, 2 * (n0 + u + 1))
                    sp.dma_start(unit_rows(xl_tab[nxt], u), projected[:, s, :, 0:C]).then_inc(row_out[s], 16)
                    sp.dma_start(unit_rows(xr_tab[nxt], u), projected[:, s, :, C:2 * C]).then_inc(row_out[s], 16)

                sp.wait_ge(add_done[1], ROUNDS * (layer + 1) + 1)
                if layer == 0:
                    unit_loop(sp, [(0, fetch), (9, store_norm), (13, store_proj)])
                elif layer < GAT:
                    unit_loop(sp, [(0, fetch), (8, store_proj)])
                else:
                    unit_loop(sp, [(0, fetch), (9, store_norm)])

            for layer in range(LAYERS):
                edge_phase(layer)
                node_phase(layer)
            for s in range(4):
                sp.wait_ge(norm_out[s], PER_LAYER)

        @block.gpsimd
        def _(pool):
            g = nc.gpsimd
            g.memset(ident[:, :], 0.0).then_inc(consts, 1)
            g.memset(zeros_b[:, :], 0.0).then_inc(consts, 1)
            g.memset(zero_row[:, :], 0.0).then_inc(consts, 1)
            g.memset(ones_b, 1.0).then_inc(consts, 1)
            g.memset(mean_c, 0.0).then_inc(consts, 1)
            g.iota(iota_i, pattern=[[1, P]], base=0, channel_multiplier=0).then_inc(consts, 1)
            g.iota(pid_i, pattern=[[0, 1]], base=0, channel_multiplier=1).then_inc(consts, 1)
            g.iota(tile_i, pattern=[[SELP, SELQ]], base=0, channel_multiplier=1).then_inc(consts, 1)
            g.iota(chunk_k, pattern=[[CH, NCH]], base=CH, channel_multiplier=0).then_inc(consts, 1)
            g.iota(round_i, pattern=[[0, NCH], [PAIRS, ROUNDS]], base=PAIRS,
                   channel_multiplier=0).then_inc(consts, 1)
            g.iota(k_i, pattern=[[1, K]], base=0, channel_multiplier=0).then_inc(consts, 1)
            pool.wait_ge(consts, 11)
            g.affine_select(out=ident[:, :], in_=ident[:, :], compare_op=ALU.not_equal, fill=1.0,
                            base=0, pattern=[[-1, P]], channel_multiplier=1).then_inc(consts, 1)
            pool.wait_ge(consts, 12)
            g.memset(mean_c[R:R + 1, C:C + 1], 1.0).then_inc(consts, 1)

            pool.wait_ge(prep_v, PV["fold"])

            def edge_phase(layer):
                table = io["x"] if layer == 0 else xl_tab[(layer - 1) % 2]

                def body(it, k):
                    kk = k + NCH * layer
                    waits_apart(pool, consts, (idx_in[kk % 4], 16 * (it + kk // 4 + 1)),
                                (msg_done, 4 * it + kk - 1))
                    for t in range(CH):
                        q = (kk % 2) * QCH + t // QUAD
                        pool.indirect_dma_start(
                            gathered[:, kk % 2, t, :], None, table,
                            bass.IndirectOffsetOnAxis(edge_idx[:, kk % 4, 0, t:t + 1], 0),
                        ).then_inc(gat_in[q], 16)
                        if layer:
                            pool.indirect_dma_start(
                                gathered_r[:, kk % 2, t, :], None, xr_tab[(layer - 1) % 2],
                                bass.IndirectOffsetOnAxis(edge_idx[:, kk % 4, 1, t:t + 1], 0),
                            ).then_inc(gat_in[q], 16)
                if layer:
                    for s in range(4):
                        pool.wait_ge(row_out[s], PER_LAYER * layer)
                        pool.wait_ge(norm_out[s], PER_LAYER // 2)
                    pool.wait_ge(s_score, UNITS * layer)
                chunk_loop(pool, body, layer)

            def node_phase(layer):
                n0 = UNITS * (layer - 1)

                def clear(u, s, n):
                    if layer == 0:
                        pool.wait_ge(copy_done, u + 1)
                    else:
                        pool.wait_ge(edge_part, n0 + u + 1)
                    g.tensor_copy(nodes[:, ds(QUAD * u, QUAD), :],
                                  zero_row[:, None, :].to_broadcast([P, QUAD, NW])).then_inc(cleared, 1)

                def self_share(u, s, n):
                    pool.wait_ge(row_in[s], 16 * ((UNITS // 4) * layer + n))
                    w(pool, h_done, n0 + u - 3)
                    ins = g.tensor_tensor(t_self[:, s], loaded[:, s],
                                          c_self[:, ds(QUAD * u, QUAD)][:, :, None].to_broadcast([P, QUAD, C]),
                                          ALU.mult)
                    if layer < GAT:
                        ins.then_inc(self_part, 1)
                        return
                    ins.then_inc(res_added, 1)
                    res = projected[:, s, :, 0:C]
                    pool.wait_ge(res_in[s], 16 * n)
                    g.tensor_tensor(res, res, bias_b[:, None, :].to_broadcast([P, QUAD, C]),
                                    ALU.add).then_inc(res_added, 1)
                    pool.wait_ge(res_added, 2 * (u + 1))
                    g.tensor_tensor(t_self[:, s], t_self[:, s], res, ALU.add).then_inc(self_part, 1)

                def add_bias(u, s, n):
                    pool.wait_ge(row_in[s], 16 * n)
                    g.tensor_tensor(loaded[:, s], loaded[:, s], bias0_b[:, None, :].to_broadcast([P, QUAD, C]),
                                    ALU.add).then_inc(row_biased, 1)

                if layer == 0:
                    unit_loop(pool, [(1, clear), (2, add_bias)])
                else:
                    pool.wait_ge(coef_v, 10 * layer)
                    unit_loop(pool, [(2, self_share)] + ([(3, clear)] if layer < GAT else []))

            for layer in range(LAYERS):
                edge_phase(layer)
                node_phase(layer)

        @block.tensor
        def _(pe):
            mm, tr = nc.tensor.matmul, nc.tensor.transpose
            pe.wait_ge(prep_v, PV["before"])
            for half in range(2):
                for q in range(SELQ):
                    last = mm(bank[half][:, 0:HK], ones_b[:, :], before[:, q, half * HK:(half + 1) * HK],
                              start=q == 0, stop=q == SELQ - 1)
            last.then_inc(prep_t, 1)
            pe.wait_ge(prep_v, PV["pick"])
            for half in range(2):
                for q in range(SELQ):
                    last = mm(bank[2 + half][:, 0:HK], drow[:, q, :], pick[:, q, half * HK:(half + 1) * HK],
                              start=q == 0, stop=q == SELQ - 1)
            last.then_inc(prep_t, 1)
            pe.wait_ge(prep_v, PV["fold"])
            mm(bank[4][0:R, 0:1], fold, attr_sum, start=True, stop=True)
            for n in range(GAT):
                last = mm(bank[5][0:R + 1, n * C:(n + 1) * C], emb_t, we_in[:, n, :], start=True, stop=True)
            last.then_inc(prep_t, 1)
            pe.wait_ge(prep_v, PV["we"])
            for n in range(GAT):
                last = mm(bank[6][0:C + 1, n * C:(n + 1) * C], mean_c, we[:, n, 0:C], start=True, stop=True)
            last.then_inc(prep_t, 1)

            def rounds(layer, c):
                lo = pe.value_load(round_tab[0:1, ds(c, 1)], min_val=0, max_val=ROUNDS)
                hi = pe.value_load(round_tab[0:1, ds(c + 1, 1)], min_val=0, max_val=ROUNDS)
                with pe.Fori(lo, hi) as r:
                    g = r + (ROUNDS * layer + 1)
                    ring, off = (nc.values_load_multi_w_load_instructions(
                        pair_tab[0:1, ds(r, 1), 2 * x:2 * x + 2, :].rearrange("p o a b -> p (o a b)"),
                        engines=(PE,), min_val=0, max_val=most,
                        skip_runtime_bounds_check_because=CLAMPED)[1]
                        for x, most in enumerate((4 * CH - 1, STEPS - 1)))
                    for b in range(2):
                        pe.wait_ge(add_done[b], g)
                        mm(win_ps[b][:, 0:STEPS * W], zeros_b[:, 0:P], zeros_b[:, 0:STEPS * W],
                           start=True, stop=True, skip_group_check=True)
                        pe.wait_ge(hot_done[b], g + 1)
                        for s in range(STEPS):
                            last = mm(win_ps[b][:, ds(off[b * STEPS + s] * W, W)], hot[b][:, s, :],
                                      msg[:, ds(ring[b * STEPS + s], 1), :].rearrange("p o w -> p (o w)"),
                                      start=False, stop=True, skip_group_check=True)
                        last.then_inc(win_done[b], 1)

            def carry(layer, it, k):
                kk = k + NCH * layer
                n = 4 * it + kk
                if isinstance(it, int) and k == 0:
                    pe.wait_ge(msg_done, n + 1)
                w(pe, carried, 4 * it + k + (NCH - 1) * layer)
                pe.wait_ge(cross_done, n + 1)
                for t in range(CH):
                    last = mm(carry_ps[0:1, 0:W], cross_ring[:, kk % 2, t:t + 1],
                              msg[:, (k % 4) * CH + t, :], start=t == 0, stop=t == CH - 1)
                last.then_inc(carry_done, 1)

            def edge_phase(layer):
                def scores(it, k):
                    kk = k + NCH * layer
                    n1 = 4 * it + k + NCH * (layer - 1)
                    for q in range(QCH):
                        nq = 4 * n1 + q
                        pe.wait_ge(attr_in[q], 16 * (n1 + 1))
                        w(pe, z_read, nq - 1)
                        for t in range(QUAD):
                            last = mm(z_ps[q % 2][:, t * Y:(t + 1) * Y], attr[:, q, t * P:(t + 1) * P],
                                      we[:, layer - 1, :], start=t == 0, stop=True, skip_group_check=True)
                        last.then_inc(z_done, 1)
                    waits_apart(pe, consts, (score_done, QCH * (n1 + 1)))
                    tr(tr_ps[0:CH, 0:P], score[:, kk % 2, :], ident[:, :]).then_inc(score_t, 1)
                    waits_apart(pe, consts, (scans, 2 * (n1 + 1)))
                    tr(row_ps[0:1, 0:CH], scan_f[:, P - 1:P], ident[0:CH, 0:CH])
                    tr(row_ps[0:1, CH:2 * CH], scan_b[:, 0:1], ident[0:CH, 0:CH]).then_inc(ends_t, 1)
                    waits_apart(pe, consts, (rows_done, 3 * (n1 + 1)))
                    tr(row_ps[0:CH, 32:33], fwd_row[:, kk % 2, 0:CH], ident[0:1, 0:1])
                    tr(row_ps[0:CH, 33:34], bwd_row[:, 1:CH + 1], ident[0:1, 0:1]).then_inc(rows_t, 1)
                    waits_apart(pe, consts, (max_done, n1 + 1))
                    tr(row_ps[:, 64:64 + CH], seg_max[:, :], ident[0:CH, 0:CH]).then_inc(max_t, 1)

                def body(it, k):
                    if layer:
                        scores(it, k)
                    carry(layer, it, k)
                    rounds(layer, 4 * it + k)

                if layer:
                    pe.wait_ge(proj_copied, 2 * UNITS * layer)
                chunk_loop(pe, body, layer)

            def node_phase(layer):
                n0 = UNITS * layer

                def turned(to, t, rows):
                    return mm(to[0:C, t * P:(t + 1) * P], rows, ident[:, :], start=t == 0, stop=True,
                              skip_group_check=True)

                def f_transpose(u, s, n):
                    waits_apart(pe, consts, (copy_done, u + 1), (f_t_copied, u))
                    for pair in range(2):
                        last = mm(ht_ps[0][:, pair * P:(pair + 1) * P],
                                  sums[:, s % 2, 2 * pair:2 * pair + 2, :].rearrange("p t c -> p (t c)"),
                                  ident[:, :], start=pair == 0, stop=True, skip_group_check=True)
                    last.then_inc(f_t, 1)

                def y(u, s, n):
                    pe.wait_ge(f_t_copied, u + 1)
                    pe.wait_ge(row_biased, u + 1)
                    w(pe, center_done, u - 1)
                    for pair in range(2):
                        mm(y_ps[s % 2][:, pair * 2 * C:(pair + 1) * 2 * C], f_cols[:, s % 2, pair, :],
                           w0[:, :], start=pair == 0, stop=True, skip_group_check=True)
                    mm(y_ps[s % 2][:, 0:QUAD * C], ident[:, :], loaded[:, s].rearrange("p a b -> p (a b)"),
                       start=False, stop=True, skip_group_check=True).then_inc(y_done, 1)

                def h_transpose(u, s, n):
                    if layer == 0:
                        waits_apart(pe, consts, (norm_done, u + 1), (h_t_copied, u))
                    else:
                        waits_apart(pe, consts, (h_done, n0 - UNITS + u + 1), (h_t_copied, n0 + u - 1))
                    for t in range(QUAD):
                        last = turned(ht_ps[1 if layer == 0 else s % 2], t, h[:, s, t, :])
                    last.then_inc(h_t_done, 1)

                def project(u, s, n):
                    pe.wait_ge(h_t_copied, n0 + u + 1)
                    w(pe, proj_copied, 2 * (n0 + u - 1))
                    for t in range(QUAD):
                        last = mm(pj_ps[2 * (s % 2) + t // 2][:, t % 2 * PROJ:(t % 2 + 1) * PROJ],
                                  h_t[:, s % 2, t * P:(t + 1) * P], pw[:, layer, :],
                                  start=t % 2 == 0, stop=t % 2 == 1, skip_group_check=True)
                    last.then_inc(proj_done, 1)

                pe.wait_ge(add_done[1], ROUNDS * (layer + 1) + 1)
                pe.wait_ge(ones_set, min(layer + 1, GAT))
                if layer == 0:
                    unit_loop(pe, [(3, y), (11, project), (1, f_transpose), (9, h_transpose)])
                elif layer < GAT:
                    unit_loop(pe, [(6, project), (4, h_transpose)])

            for layer in range(LAYERS):
                edge_phase(layer)
                node_phase(layer)

        @block.scalar
        def _(act):
            a = nc.scalar.activation
            zero_c = zero_row[:, 0:1]
            act.wait_ge(consts, 13)
            act.wait_ge(prep_v, PV["we"])
            act.wait_ge(prep_t, 3)
            a(scratch[:, 0:early_end], zero_c.to_broadcast([P, early_end]), ACT.Copy).then_inc(zeroed, 1)
            act.wait_ge(prep_t, 4)
            act.wait_ge(prep_v, PV["temps"])
            a(scratch[:, early_end:late_mid], zero_c.to_broadcast([P, late_mid - early_end]),
              ACT.Copy).then_inc(zeroed, 1)
            act.wait_ge(prep_v, PV["all"])

            def edge_phase(layer):
                def body(it, k):
                    kk = k + NCH * layer
                    n = 4 * it + kk
                    n1 = n - NCH
                    ring = (k % 4) * CH
                    if layer:
                        act.wait_ge(arg_done, n1 + 1)
                        w(act, carried, 4 * it + k - 1 + (NCH - 1) * layer)
                        a(rescale[:, :], neg_arg[:, :], ACT.Exp, scale=-1.0).then_inc(rescale_done, 1)
                        act.wait_ge(less_done, n1 + 1)
                        w(act, carry_done, n - 1)
                        a(msg[:, ring:ring + CH, WGT], less_max[:, :], ACT.Exp).then_inc(exp_done, 1)
                    else:
                        w(act, carry_done, n - 1)
                        for t in range(CH):
                            if t % QUAD == 0:
                                act.wait_ge(gat_in[kk % 2 * QCH + t // QUAD],
                                            gath_target(0, it, k, t // QUAD))
                            last = a(msg[:, ring + t, 0:C], gathered[:, kk % 2, t, :], ACT.Copy,
                                     scale=weight[:, ds((4 * it + k) * CH + t, 1)])
                        last.then_inc(msg_done, 1)

                if layer:
                    act.wait_ge(win_done[1], ROUNDS * layer + 1)
                chunk_loop(act, body, layer)

            def node_phase(layer):
                n0 = UNITS * layer
                ln0 = 0 if layer == 0 else UNITS

                def copy_sums(u, s, n):
                    w(act, f_t, u - 1)
                    a(sums[:, s % 2], nodes[:, ds(QUAD * u, QUAD), 0:C], ACT.Copy).then_inc(copy_done, 1)

                def f_copy(u, s, n):
                    act.wait_ge(f_t, u + 1)
                    w(act, y_done, u - 1)
                    a(f_cols[:, s % 2].rearrange("p a b -> p (a b)"), ht_ps[0][:, 0:2 * P], ACT.Copy).then_inc(f_t_copied, 1)

                def square(u, s, n):
                    act.wait_ge(center_done, ln0 + u + 1)
                    w(act, var_done, ln0 + u - 1)
                    a(squares[:, s % 2], centered[layer // GAT][:, s], ACT.Square).then_inc(square_done, 1)

                def deviation(u, s, n):
                    act.wait_ge(var_done, ln0 + u + 1)
                    a(stat[:, s, 2], stat[:, s, 1], ACT.Sqrt, bias=eps_c[:, 0:1], scale=1.0 / C).then_inc(dev_done, 1)

                def h_copy(u, s, n):
                    act.wait_ge(h_t_done, n0 + u + 1)
                    w(act, proj_done, n0 + u - 1)
                    if layer:
                        a(h_t[0:C, s % 2, :], ht_ps[s % 2][0:C, :], ACT.Relu,
                          bias=bias_c[:, layer - 1:layer]).then_inc(h_t_copied, 1)
                    else:
                        a(h_t[0:C, s % 2, :], ht_ps[1][0:C, :], ACT.Copy).then_inc(h_t_copied, 1)

                def proj_copy(u, s, n):
                    act.wait_ge(proj_done, n0 + u + 1)
                    w(act, s_leaky, n0 + u - 3)
                    w(act, row_out[s], PER_LAYER * layer + 32 * (n - 1))
                    for b in range(2):
                        a(projected[:, s, 2 * b:2 * b + 2, :],
                          pj_ps[2 * (s % 2) + b][:, 0:2 * PROJ].rearrange("p (t c) -> p t c", t=2),
                          ACT.Copy).then_inc(proj_copied, 1)

                if layer:
                    act.wait_ge(coef_v, 10 * (layer - 1) + 4)
                    a(c_edge[:, :], c_edge[:, :], ACT.Exp).then_inc(coef_a, 1)
                    a(c_self[:, :], c_self[:, :], ACT.Exp).then_inc(coef_a, 1)
                else:
                    act.wait_ge(add_done[1], ROUNDS + 1)
                    act.wait_ge(msg_done, NCH)
                if layer == 0:
                    unit_loop(act, [(2, f_copy), (10, h_copy), (5, square), (7, deviation),
                                    (12, proj_copy), (0, copy_sums)])
                elif layer < GAT:
                    unit_loop(act, [(5, h_copy), (7, proj_copy)])
                else:
                    unit_loop(act, [(7, deviation), (5, square)])

            for layer in range(LAYERS):
                edge_phase(layer)
                node_phase(layer)

        @block.vector
        def _(dve):
            v = nc.vector
            step = [0]

            def seq(ins):
                step[0] += 1
                ins.then_inc(prep_v, 1)
                dve.wait_ge(prep_v, step[0])

            if late_end < NT * NW:
                v.memset(scratch[:, late_end:], 0.0)
            v.memset(spare[:, 2 * NCH * ROUNDS:], 0.0)
            dve.wait_ge(loads, 16 * N_LOADS)
            dve.wait_ge(consts, 13)
            seq(v.tensor_copy(iota_f[:, :], iota_i))
            seq(v.tensor_copy(part_id[:, :], pid_i))
            seq(v.tensor_copy(k_f, k_i))
            seq(v.tensor_copy(tile_f, tile_i))
            seq(v.tensor_scalar(last_i, last_i, 7, None, ALU.logical_shift_right))
            seq(v.tensor_copy(v_f, last_i))
            seq(v.tensor_scalar(v_f, v_f, float(NTR - 1), None, ALU.min))
            seq(v.tensor_tensor(v_f, v_f, tile_f[0:SELP], ALU.add))
            for q in range(SELQ):
                seq(v.tensor_scalar(before[:, q, :], k_f[0:SELP], v_f[:, q:q + 1], None, ALU.is_gt))
            assert step[0] == PV["before"]
            seq(v.tensor_tensor(drow, rows_i[:, 0], rows_i[:, 1], ALU.is_equal))
            seq(v.tensor_tensor(drow2, rows_i[:, 1], rows_i[:, 2], ALU.is_equal))
            seq(v.tensor_tensor(drow, drow, drow2, ALU.mult))
            seq(v.tensor_scalar(drow, drow, float(FAR), None, ALU.mult))
            seq(v.tensor_tensor(drow, drow, rows_i[:, 0], ALU.add))
            dve.wait_ge(prep_t, 1)
            for half in range(2):
                seq(v.tensor_scalar(ik_f[:, half * HK:(half + 1) * HK], bank[half][:, 0:HK],
                                    float(ET - 1), None, ALU.min))
            for q in range(SELQ):
                seq(v.tensor_scalar(pick[:, q, :], ik_f[0:SELP], tile_f[0:SELP, q:q + 1], None, ALU.is_equal))
            assert step[0] == PV["pick"]
            seq(v.tensor_tensor(jk_f, k_f, ik_f, ALU.subtract))
            seq(v.tensor_scalar(jk_f, jk_f, float(NTR - 1), None, ALU.min))
            dve.wait_ge(attr_loads, 16 * 8)
            seq(v.tensor_reduce(attr_sum, attr_a, AX, ALU.add))
            seq(v.tensor_reduce(attr_sum2, attr_b, AX, ALU.add))
            seq(v.tensor_tensor(attr_sum, attr_sum, attr_sum2, ALU.add))
            seq(v.tensor_tensor(fold, ident[:, 0:R], ident[:, R:2 * R], ALU.add))
            seq(v.tensor_tensor(fold, fold, ident[:, 2 * R:3 * R], ALU.add))
            seq(v.tensor_tensor(fold, fold, ident[:, 3 * R:4 * R], ALU.add))
            assert step[0] == PV["fold"]
            dve.wait_ge(prep_t, 3)
            seq(v.tensor_scalar(mean_c[0:R, C:C + 1], bank[4][0:R, 0:1], 1.0 / E, None, ALU.mult))
            seq(v.tensor_copy(we[:, :, 0:C], bank[5][0:R + 1, 0:GAT * C].rearrange("p (a b) -> p a b", a=GAT)))
            assert step[0] == PV["we"]
            for half in range(2):
                sl = slice(half * HK, (half + 1) * HK)
                seq(v.scalar_tensor_tensor(out=dst_rel[:, sl], in0=jk_f[:, sl], scalar=float(-P),
                                           in1=bank[2 + half][:, 0:HK], op0=ALU.mult, op1=ALU.add))
            seq(v.tensor_copy(dst_rel[:, K:], dst_rel[:, 0:PAIRS]))
            seq(v.tensor_copy(ring_i, ik_f[0:1]))
            seq(v.tensor_scalar(ring_i, ring_i, 4 * CH - 1, None, ALU.bitwise_and))
            seq(v.memset(pair_tab[:, :, :, :], 0))
            seq(v.tensor_copy(pair_tab[:, :, 0:2, 0:STEPS], ring_i.rearrange("p (a b c) -> p a b c", b=2, c=STEPS)))
            j4 = jk_f[0:1].rearrange("p (a b c) -> p a b c", b=2, c=STEPS)
            seq(v.tensor_copy(tile_tab[:, :, 0:2], j4[:, :, :, 0]))
            seq(v.tensor_tensor(ik_f[0:1].rearrange("p (a b c) -> p a b c", b=2, c=STEPS), j4,
                                j4[:, :, :, 0:1].to_broadcast([1, ROUNDS, 2, STEPS]), ALU.subtract))
            seq(v.tensor_copy(pair_tab[:, :, 2:4, 0:STEPS],
                              ik_f[0:1].rearrange("p (a b c) -> p a b c", b=2, c=STEPS)))
            seq(v.tensor_scalar(chunk_i[:, 0], chunk_i[:, 0], 7, None, ALU.logical_shift_right))
            seq(v.tensor_copy(chunk_f, chunk_i[:, 0]))
            seq(v.tensor_scalar(chunk_f, chunk_f, float(NTR - 1), None, ALU.min))
            seq(v.tensor_tensor(chunk_f, chunk_f, chunk_k, ALU.add))
            seq(v.tensor_copy(round_c, round_i))
            seq(v.tensor_tensor(round_c, round_c, chunk_f[:, :, None].to_broadcast([1, NCH, ROUNDS]), ALU.is_le))
            seq(v.tensor_reduce(round_f, round_c, AX, ALU.add))
            seq(v.memset(round_tab[:, :], 0))
            seq(v.tensor_copy(round_tab[:, 1:NCH + 1], round_f))
            seq(v.memset(round_tab[:, NCH:NCH + 1], ROUNDS))
            seq(v.tensor_tensor(goes_on[:, :], chunk_i[:, 1], chunk_i[:, 2], ALU.is_equal))
            seq(v.tensor_tensor(win_f, win_i[:, :, 1:P + 2], win_i[:, :, 0:P + 1], ALU.is_equal))
            seq(v.tensor_scalar(same_prev[:, :, :], win_f[:, :, 0:P], 1.0, BIG, ALU.subtract, ALU.mult))
            seq(v.tensor_scalar(same_next[:, :, :], win_f[:, :, 1:P + 1][:, :, ::-1], 1.0, BIG,
                                ALU.subtract, ALU.mult))
            seq(v.tensor_tensor(row_f[:, :], ends_i[:, 0, 1:], ends_i[:, 0, :ET], ALU.is_equal))
            seq(v.tensor_scalar(row_f[:, :], row_f[:, :], 1.0, BIG, ALU.subtract, ALU.mult))
            seq(v.tensor_tensor(ends_f, ends_i[:, 1, 1:], ends_i[:, 1, :ET], ALU.is_equal))
            seq(v.tensor_scalar(row_b[:, :].rearrange("p (c t) -> p c t", t=CH),
                                ends_f.rearrange("p (c t) -> p c t", t=CH)[:, :, ::-1], 1.0, BIG,
                                ALU.subtract, ALU.mult))
            seq(v.tensor_tensor(last_edge[:, :], cols_i[:, 0], cols_i[:, 1], ALU.not_equal))
            seq(v.tensor_tensor(ccol[:, 0], cols_i[:, 0], cols_i[:, 2], ALU.is_equal))
            seq(v.tensor_tensor(ccol[:, 1], cols_i[:, 2], cols_i[:, 3], ALU.is_equal))
            seq(v.tensor_tensor(crosses[:, :], ccol[:, 0], ccol[:, 1], ALU.mult))
            dve.wait_ge(prep_t, 4)
            seq(v.tensor_tensor(pw[:, :, 2 * C:], pw[:, :, 0:C], pw[:, :, C:2 * C], ALU.add))
            seq(v.tensor_tensor(pw[:, :, 2 * C:], pw[:, :, 2 * C:],
                                bank[6][0:C + 1, 0:GAT * C].rearrange("p (a b) -> p a b", a=GAT), ALU.add))
            seq(v.memset(we[:, :, C:], 0.0))
            seq(v.memset(bwd_row[:, :], -BIG))
            seq(v.memset(eps_c[:, :], EPS))
            seq(v.memset(w0[0:C, C:], 0.0))
            seq(v.memset(w0[C:, 0:C], 0.0))
            for s in (*hot_done, *win_done, *add_done):
                v.memset(less_max[:, 0:1], 0.0).then_inc(s, 1)
                dve.wait_ge(s, 1)
            assert step[0] == PV["temps"], step
            seq(v.memset(spare[:, 0:2 * NCH * ROUNDS], 0.0))
            seq(v.memset(scratch[:, late_mid:late_end], 0.0))
            assert step[0] == PV["all"], step

            def rounds(layer, c):
                lo = dve.value_load(round_tab[0:1, ds(c, 1)], min_val=0, max_val=ROUNDS)
                hi = dve.value_load(round_tab[0:1, ds(c + 1, 1)], min_val=0, max_val=ROUNDS)
                with dve.Fori(lo, hi) as r:
                    g = r + (ROUNDS * layer + 1)
                    _, first = nc.values_load_multi_w_load_instructions(
                        tile_tab[0:1, ds(r, 1), 0:2].rearrange("p a b -> p (a b)"),
                        engines=(DVE,), min_val=0, max_val=NTR - 1,
                        skip_runtime_bounds_check_because=CLAMPED)
                    for b in range(2):
                        dve.wait_ge(win_done[b], g + 1)
                        dve.wait_ge(add_done[1 - b], g + b)
                        table = nodes[:, ds(first[b], STEPS), :]
                        v.tensor_tensor(table, table,
                                        win_ps[b][:, 0:STEPS * W].rearrange("p (t w) -> p t w", t=STEPS)[:, :, 0:NW],
                                        ALU.add).then_inc(add_done[b], 1)
                        dve.wait_ge(hot_done[b], g + 1)
                        one_hot(b, r * PAIRS + (PAIRS + b * STEPS))

            def one_hot(b, first_pair):
                v.tensor_tensor(hot[b][:, :, :], iota_f[:, None, :].to_broadcast([P, STEPS, P]),
                                dst_rel[:, ds(first_pair, STEPS)][:, :, None].to_broadcast([P, STEPS, P]),
                                ALU.is_equal).then_inc(hot_done[b], 1)

            def edge_phase(layer):
                def scores(it, k):
                    kk = k + NCH * layer
                    n1 = 4 * it + kk - NCH
                    c = 4 * it + k
                    def both(q, nq):
                        dve.wait_ge(gat_in[kk % 2 * QCH + q], gath_target(layer, it, k, q))
                        v.tensor_tensor(z_of(q), gathered[:, kk % 2, q * QUAD:(q + 1) * QUAD, :], z_of(q),
                                        ALU.add).then_inc(sum_done, 1)

                    def z_of(q):
                        return gathered_r[:, kk % 2, q * QUAD:(q + 1) * QUAD, :]

                    def with_attr(q, nq):
                        dve.wait_ge(sum_done, nq + 1)
                        dve.wait_ge(z_done, nq + 1)
                        v.tensor_tensor(z_of(q), z_of(q), z_ps[q % 2][:, 0:QUAD * Y].rearrange(
                            "p (t c) -> p t c", t=QUAD)[:, :, 0:C], ALU.add).then_inc(z_read, 1)

                    def leaky(q, nq):
                        dve.wait_ge(z_read, nq + 1)
                        v.scalar_tensor_tensor(out=leaky_e[:, q], in0=z_of(q), scalar=SLOPE, in1=z_of(q),
                                               op0=ALU.mult, op1=ALU.max).then_inc(leaky_done, 1)

                    def times_att(q, nq):
                        dve.wait_ge(leaky_done, nq + 1)
                        v.tensor_tensor(weighted_e[:, q], leaky_e[:, q],
                                        att_b[:, layer - 1:layer, :].to_broadcast([P, QUAD, C]),
                                        ALU.mult).then_inc(att_done, 1)

                    def total(q, nq):
                        dve.wait_ge(att_done, nq + 1)
                        w(dve, less_done, n1 - 1)
                        v.tensor_reduce(score[:, kk % 2, q * QUAD:(q + 1) * QUAD], weighted_e[:, q],
                                        AX, ALU.add).then_inc(score_done, 1)

                    steps = (both, with_attr, leaky, times_att, total)
                    for x in range(QCH + len(steps) - 1):
                        for s in range(len(steps) - 1, -1, -1):
                            if 0 <= x - s < QCH:
                                steps[s](x - s, 4 * n1 + x - s)
                    dve.wait_ge(score_t, n1 + 1)
                    w(dve, scans2, 2 * n1)
                    w(dve, max_done, n1)
                    flags_f = same_prev[:, ds(c, 1), :].rearrange("p a b -> p (a b)")
                    flags_b = same_next[:, ds(c, 1), :].rearrange("p a b -> p (a b)")
                    st = tr_ps[0:CH, 0:P]
                    v.tensor_tensor_scan(scan_f[:, :], flags_f, st, -BIG, ALU.add, ALU.max).then_inc(scans, 1)
                    v.tensor_tensor_scan(scan_b[:, :][:, ::-1], flags_b, st[:, ::-1], -BIG, ALU.add,
                                         ALU.max).then_inc(scans, 1)
                    here, other = fwd_row[:, kk % 2], fwd_row[:, 1 - kk % 2]
                    w(dve, arg_done, n1)
                    w(dve, rows_done, 3 * n1)
                    if isinstance(it, int) and k == 0:
                        v.memset(here[:, 0:1], -BIG).then_inc(rows_done, 1)
                    else:
                        v.tensor_copy(here[:, 0:1], other[:, CH:CH + 1]).then_inc(rows_done, 1)
                    dve.wait_ge(ends_t, n1 + 1)
                    v.tensor_tensor_scan(bwd_row[:, 0:CH][:, ::-1], row_b[:, ds(c * CH, CH)],
                                         row_ps[0:1, CH:2 * CH][:, ::-1], -BIG, ALU.add,
                                         ALU.max).then_inc(rows_done, 1)
                    dve.wait_ge(rows_done, 3 * n1 + 1)
                    v.tensor_tensor_scan(here[:, 1:CH + 1], row_f[:, ds(c * CH, CH)],
                                         row_ps[0:1, 0:CH], here[:, 0:1], ALU.add, ALU.max).then_inc(rows_done, 1)
                    dve.wait_ge(rows_t, n1 + 1)
                    dve.wait_ge(scans, 2 * (n1 + 1))
                    v.tensor_copy(init[:, :], row_ps[0:CH, 32:34]).then_inc(init_done, 1)
                    dve.wait_ge(init_done, n1 + 1)
                    v.tensor_tensor_scan(scan_f[:, :], flags_f, st, init[:, 0:1], ALU.add, ALU.max).then_inc(scans2, 1)
                    v.tensor_tensor_scan(scan_b[:, :][:, ::-1], flags_b, st[:, ::-1], init[:, 1:2], ALU.add,
                                         ALU.max).then_inc(scans2, 1)
                    dve.wait_ge(scans2, 2 * (n1 + 1))
                    w(dve, max_t, n1)
                    v.tensor_tensor(seg_max[:, :], scan_f[:, :], scan_b[:, :], ALU.max).then_inc(max_done, 1)
                    dve.wait_ge(max_done, n1 + 1)
                    w(dve, rescale_done, n1)
                    v.scalar_tensor_tensor(out=neg_arg[:, :], in0=seg_max[0:1, 0:1], scalar=here[:, 0:1],
                                           in1=goes_on[:, ds(c, 1)], op0=ALU.subtract,
                                           op1=ALU.mult).then_inc(arg_done, 1)
                    dve.wait_ge(max_t, n1 + 1)
                    w(dve, exp_done, n1)
                    top = row_ps[:, 64:64 + CH]
                    v.tensor_tensor(less_max[:, :], score[:, kk % 2, :], top, ALU.subtract).then_inc(less_done, 1)
                    w(dve, carry_done, 4 * it + kk - 1)
                    ring = (k % 4) * CH
                    flag = last_edge[:, ds(c * CH, CH)]
                    v.tensor_copy(msg[:, ring:ring + CH, LAST], flag).then_inc(flags_done, 1)
                    v.tensor_tensor(msg[:, ring:ring + CH, MAXI], flag, top, ALU.mult).then_inc(flags_done, 1)
                    dve.wait_ge(exp_done, n1 + 1)
                    for q in range(QCH):
                        rows = msg[:, ring + q * QUAD:ring + (q + 1) * QUAD, :]
                        last = v.tensor_tensor(rows[:, :, 0:C], gathered[:, kk % 2, q * QUAD:(q + 1) * QUAD, :],
                                               rows[:, :, WGT:WGT + 1].to_broadcast([P, QUAD, C]), ALU.mult)
                    last.then_inc(msg_done, 1)

                def body(it, k):
                    kk = k + NCH * layer
                    n = 4 * it + kk
                    c = 4 * it + k
                    first = isinstance(it, int) and k == 0
                    if layer:
                        scores(it, k)
                    w(dve, carry_done, n - 1)
                    v.tensor_copy(cross_ring[:, kk % 2, :], crosses[:, ds(c * CH, CH)]).then_inc(cross_done, 1)
                    if not first:
                        dve.wait_ge(msg_done, n + 1)
                        dve.wait_ge(carry_done, n)
                        if layer:
                            dve.wait_ge(rescale_done, n - NCH + 1)
                        ring = (k % 4) * CH
                        v.scalar_tensor_tensor(out=msg[0:1, ring, 0:C + 1], in0=carry_ps[0:1, 0:C + 1],
                                               scalar=rescale[:, 0:1] if layer else 1.0,
                                               in1=msg[0:1, ring, 0:C + 1], op0=ALU.mult,
                                               op1=ALU.add).then_inc(carried, 1)
                    rounds(layer, c)

                if layer:
                    dve.wait_ge(cleared, UNITS * layer)
                chunk_loop(dve, body, layer)

            def node_phase(layer):
                n0 = UNITS * layer
                nn = UNITS * (layer - 1)
                ln0 = 0 if layer == 0 else UNITS

                def coefficients():
                    base = [10 * (layer - 1)]

                    def cs(ins):
                        base[0] += 1
                        ins.then_inc(coef_v, 1)
                        dve.wait_ge(coef_v, base[0])
                    t1 = region[:, 0:NT]
                    t2 = region[:, NT:2 * NT]
                    dve.wait_ge(add_done[0], ROUNDS * (layer + 1) + 1)
                    dve.wait_ge(add_done[1], ROUNDS * (layer + 1) + 1)
                    cs(v.tensor_scalar(t1, nodes[:, :, LAST], BIG, BIG, ALU.mult, ALU.subtract))
                    cs(v.tensor_tensor(t1, t1, nodes[:, :, MAXI], ALU.add))
                    cs(v.tensor_tensor(t2, t1, self_score[:, :], ALU.max))
                    v.tensor_tensor(c_edge[:, :], t1, t2, ALU.subtract)
                    cs(v.tensor_tensor(c_self[:, :], self_score[:, :], t2, ALU.subtract))
                    dve.wait_ge(coef_a, 2 * layer)
                    cs(v.tensor_tensor(t1, c_edge[:, :], nodes[:, :, WGT], ALU.mult))
                    cs(v.tensor_tensor(t1, t1, c_self[:, :], ALU.add))
                    cs(v.tensor_scalar(t1, t1, 1e-16, None, ALU.add))
                    cs(v.reciprocal(t2, t1))
                    cs(v.tensor_tensor(c_edge[:, :], c_edge[:, :], t2, ALU.mult))
                    cs(v.tensor_tensor(c_self[:, :], c_self[:, :], t2, ALU.mult))

                def edge_share(u, s, n):
                    if layer < GAT:
                        w(dve, h_t_done, n0 + u - 3)
                    q = ds(QUAD * u, QUAD)
                    v.tensor_tensor(h[:, s], nodes[:, q, 0:C],
                                    c_edge[:, q][:, :, None].to_broadcast([P, QUAD, C]),
                                    ALU.mult).then_inc(edge_part, 1)

                def new_rows(u, s, n):
                    dve.wait_ge(edge_part, nn + u + 1)
                    dve.wait_ge(self_part, nn + u + 1)
                    v.tensor_tensor(h[:, s], h[:, s], t_self[:, s], ALU.add).then_inc(h_done, 1)

                def rows_of(s):
                    if layer == 0:
                        return y_ps[s % 2][:, 0:QUAD * C].rearrange("p (t c) -> p t c", t=QUAD)
                    return h[:, s]

                def total(u, s, n):
                    if layer == 0:
                        dve.wait_ge(y_done, u + 1)
                    else:
                        dve.wait_ge(h_done, nn + u + 1)
                    v.tensor_reduce(stat[:, s, 0], rows_of(s), AX, ALU.add).then_inc(mean_sum, 1)

                def center(u, s, n):
                    dve.wait_ge(mean_sum, ln0 + u + 1)
                    w(dve, norm_done, ln0 + u - 3)
                    v.scalar_tensor_tensor(out=centered[layer // GAT][:, s],
                                           in0=stat[:, s, 0][:, :, None].to_broadcast([P, QUAD, C]),
                                           scalar=-1.0 / C, in1=rows_of(s), op0=ALU.mult,
                                           op1=ALU.add).then_inc(center_done, 1)

                def variance(u, s, n):
                    dve.wait_ge(square_done, ln0 + u + 1)
                    v.tensor_reduce(stat[:, s, 1], squares[:, s % 2], AX, ALU.add).then_inc(var_done, 1)

                def inverse(u, s, n):
                    dve.wait_ge(dev_done, ln0 + u + 1)
                    v.reciprocal(stat[:, s, 3], stat[:, s, 2]).then_inc(inv_done, 1)

                def scale(u, s, n):
                    dve.wait_ge(inv_done, ln0 + u + 1)
                    if layer == 0:
                        w(dve, h_t_done, u - 3)
                    w(dve, norm_out[s], (PER_LAYER // 2 if layer else 0) + 16 * (n - 1))
                    v.tensor_tensor(normed[layer // GAT][:, s], centered[layer // GAT][:, s],
                                    stat[:, s, 3][:, :, None].to_broadcast([P, QUAD, C]),
                                    ALU.mult).then_inc(norm_done, 1)

                def self_leaky(u, s, n):
                    dve.wait_ge(proj_copied, 2 * (n0 + u + 1))
                    w(dve, s_att, n0 + u - 1)
                    z = projected[:, s, :, 2 * C:]
                    v.scalar_tensor_tensor(out=leaky_s[:, s % 2], in0=z, scalar=SLOPE, in1=z, op0=ALU.mult,
                                           op1=ALU.max).then_inc(s_leaky, 1)

                def self_att(u, s, n):
                    dve.wait_ge(s_leaky, n0 + u + 1)
                    w(dve, s_score, n0 + u - 1)
                    v.tensor_tensor(weighted_s[:, s % 2], leaky_s[:, s % 2],
                                    att_b[:, layer:layer + 1, :].to_broadcast([P, QUAD, C]),
                                    ALU.mult).then_inc(s_att, 1)

                def self_sum(u, s, n):
                    dve.wait_ge(s_att, n0 + u + 1)
                    v.tensor_reduce(self_score[:, ds(QUAD * u, QUAD)], weighted_s[:, s % 2], AX,
                                    ALU.add).then_inc(s_score, 1)

                if layer < GAT:
                    v.memset(h_t[C:C + 1, :, :], 1.0).then_inc(ones_set, 1)
                if layer == 0:
                    unit_loop(dve, [(8, inverse), (4, total), (13, self_leaky), (8, scale), (13, self_att),
                                    (4, center), (6, variance), (13, self_sum)])
                elif layer < GAT:
                    coefficients()
                    unit_loop(dve, [(8, self_leaky), (2, edge_share), (8, self_att), (3, new_rows),
                                    (8, self_sum)])
                else:
                    coefficients()
                    unit_loop(dve, [(8, inverse), (4, total), (2, edge_share), (8, scale), (3, new_rows),
                                    (4, center), (6, variance)])

            for b in range(2):
                one_hot(b, b * STEPS)
            dve.wait_ge(zeroed, 2)
            for layer in range(LAYERS):
                edge_phase(layer)
                node_phase(layer)


PER_LAYER = 32 * (UNITS // 4)
PE = mybir.EngineType.PE
DVE = mybir.EngineType.DVE
PV = {"before": 12, "pick": 23, "fold": 31, "we": 33, "temps": 72, "all": 74}


def kernel(**inputs):
    import concourse.bacc as bacc
    from concourse.bass_utils import run_bass_kernel_spmd

    a = {k: np.ascontiguousarray(v) for k, v in inputs.items()}
    pad = ROWS - E

    def padded(v, fill):
        return np.pad(v, [(0, pad)] + [(0, 0)] * (v.ndim - 1), constant_values=fill)

    def columns(v):
        return np.ascontiguousarray(v.reshape(ET, P).T)

    dst, src = padded(a["dst"], FAR), padded(a["src"], 0)
    dst_g = padded(a["dst"], 0)
    after = np.concatenate([dst[1:], [-1]]).astype(np.int32)
    around = np.concatenate([[-1], dst, [-1]]).astype(np.int32)
    chunk = CH * P
    c_last = np.repeat(dst[chunk - 1::chunk], chunk)
    c_next = np.repeat(after[chunk - 1::chunk], chunk)
    start = P * (np.arange(CH)[:, None] + CH * np.arange(NCH)[None, :])
    ins = {
        "x": padded(a["x"], 0),
        "edge_idx": np.ascontiguousarray(
            np.stack([src, dst_g]).reshape(2, NCH, CH, P).transpose(1, 3, 0, 2)),
        "tile_last": np.ascontiguousarray(dst[P - 1::P].reshape(SELQ, SELP).T),
        "row_dst": dst.reshape(ET, P), "row_clast": c_last.reshape(ET, P), "row_cnext": c_next.reshape(ET, P),
        "col_ids": np.stack([columns(v) for v in (dst, after, c_last, c_next)]),
        "win_dst": around[start[:, :, None] + np.arange(P + 2)],
        "row_ends": np.stack([around[0::P][:ET + 1], around[1::P][:ET + 1]])[None],
        "chunk_ends": np.stack([dst[chunk - 1::chunk], around[0::chunk][:NCH], around[1::chunk][:NCH]])[None],
        "col_weight": columns(padded(a["edge_weight"], 0)),
        "attr_t": np.concatenate([padded(a["edge_attr_32"], 0).T, np.ones((1, ROWS), np.float32)]),
        "emb_t": np.ascontiguousarray(np.concatenate([a["L1_gnn_W_emb"], a["L1_gnn_b_emb"][None]]).T),
        "We": a["L1_gnn_We"], "Wl": a["L1_gnn_Wl"], "Wr": a["L1_gnn_Wr"], "bl": a["L1_gnn_bl"],
        "br": a["L1_gnn_br"], "W0": a["L0_gnn_W"], "b0": a["L0_gnn_b"], "att": a["L1_gnn_att"],
        "bias": a["L1_gnn_bias"], "bias_t": np.ascontiguousarray(a["L1_gnn_bias"].T),
    }
    nc = bacc.Bacc("TRN2", target_bir_lowering=False, num_devices=1)
    io = {k: nc.dram_tensor(f"in_{k}", v.shape, mybir.dt.from_np(v.dtype), kind="ExternalInput").ap()
          for k, v in ins.items()}
    io["out"] = nc.dram_tensor("out_x", (ROWS, C), F32, kind="ExternalOutput").ap()
    build(nc, io)
    r = run_bass_kernel_spmd(nc, [{f"in_{k}": v for k, v in ins.items()}], core_ids=[0])
    return r.results[0]["out_x"][:N]
```
